# Optimizing a Trainium2 kernel written in Bass

```python
import numpy as np
import jax
import jax.numpy as jnp

def _softmax(x, axis=-1):
    return jax.nn.softmax(x, axis=axis)

def _gelu(x):
    return jax.nn.gelu(x, approximate=True)

def _silu(x):
    return jax.nn.silu(x)

def _sigmoid(x):
    return jax.nn.sigmoid(x)

def _layernorm(x, axis=-1, eps=1e-05):
    m = jnp.mean(x, axis=axis, keepdims=True)
    v = jnp.var(x, axis=axis, keepdims=True)
    return (x - m) / jnp.sqrt(v + eps)

def _scatter_add(tgt, idx, src, axis=0):
    return tgt.at[idx].add(src)

def _segment_sum(src, seg, n):
    return jax.ops.segment_sum(src, seg, n)
kernel_name = 'mk_gnn_preln_d1_gnn_r64_0b2905'

def setup_inputs(seed: int=0):
    np.random.seed(seed)
    _w = jnp.asarray

    def _rec_inputs():
        import jax
        import jax.numpy as jnp
        _gk = jax.random.key(seed)
        x = -0.000202 + 1 * jax.random.normal(jax.random.fold_in(_gk, 1), (100000, 64), jnp.float32)
        src = jax.random.randint(jax.random.fold_in(_gk, 2), (50000,), 0, 100000, jnp.int32)
        dst = jax.random.randint(jax.random.fold_in(_gk, 3), (50000,), 0, 100000, jnp.int32)
        _o = jnp.argsort(dst, stable=True)
        src = src[_o]
        dst = dst[_o]
        edge_attr_16 = 0.000196303 + 1.00016 * jax.random.normal(jax.random.fold_in(_gk, 11), (50000, 16), jnp.float32)
        return (x, src, dst, edge_attr_16)
    x, src, dst, edge_attr_16 = _rec_inputs()

    def _L0_gnn_setup():
        import jax, jax.numpy as jnp
        import numpy as np
        N, E = (100000, 25000)
        IN_DIM, OUT_DIM, EDGE_DIM, H = (64, 64, 16, 4)
        HD = OUT_DIM // H
        NEG_SLOPE = 0.2
        EPS_SOFTMAX = 1e-08
        EPS_LN = 1e-05
        key = jax.random.key(seed)
        ks = jax.random.split(key, 8)
        return {'x': jax.random.normal(ks[0], (N, IN_DIM), jnp.float32), 'edge_index': jax.random.randint(ks[1], (2, E), 0, N, jnp.int64 if jax.config.jax_enable_x64 else jnp.int32), 'edge_attr': jax.random.normal(ks[2], (E, EDGE_DIM), jnp.float32), 'W_node': jax.random.normal(ks[3], (IN_DIM, OUT_DIM), jnp.float32) / np.sqrt(IN_DIM), 'W_edge': jax.random.normal(ks[4], (EDGE_DIM, H), jnp.float32) / np.sqrt(EDGE_DIM), 'attn_src': jax.random.normal(ks[5], (H, HD), jnp.float32), 'attn_dst': jax.random.normal(ks[6], (H, HD), jnp.float32), 'ln_gamma': jnp.ones((OUT_DIM,), jnp.float32), 'ln_beta': jnp.zeros((OUT_DIM,), jnp.float32)}
    _L0_gnn_all = _L0_gnn_setup()
    _L0_gnn_in = {k: v for k, v in _L0_gnn_all.items() if k in ('W_node', 'W_edge', 'attn_src', 'attn_dst', 'ln_gamma', 'ln_beta')}
    del _L0_gnn_all
    return {'x': x, 'src': src, 'dst': dst, 'edge_attr_16': edge_attr_16, 'L0_gnn_W_node': _L0_gnn_in['W_node'], 'L0_gnn_W_edge': _L0_gnn_in['W_edge'], 'L0_gnn_attn_src': _L0_gnn_in['attn_src'], 'L0_gnn_attn_dst': _L0_gnn_in['attn_dst'], 'L0_gnn_ln_gamma': _L0_gnn_in['ln_gamma'], 'L0_gnn_ln_beta': _L0_gnn_in['ln_beta']}

def reference(x, src, dst, edge_attr_16, L0_gnn_W_node, L0_gnn_W_edge, L0_gnn_attn_src, L0_gnn_attn_dst, L0_gnn_ln_gamma, L0_gnn_ln_beta):
    import jax
    import jax.numpy as jnp

    def _L0_gnn_ref(x, edge_index, edge_attr, W_node, W_edge, attn_src, attn_dst, ln_gamma, ln_beta):
        import jax, jax.numpy as jnp
        import numpy as np
        N, E = (100000, 25000)
        IN_DIM, OUT_DIM, EDGE_DIM, H = (64, 64, 16, 4)
        HD = OUT_DIM // H
        NEG_SLOPE = 0.2
        EPS_SOFTMAX = 1e-08
        EPS_LN = 1e-05
        n = x.shape[0]
        src, dst = (edge_index[0], edge_index[1])
        h = (x @ W_node).reshape(n, H, HD)
        a_src_node = jnp.einsum('nhd,hd->nh', h, attn_src)
        a_dst_node = jnp.einsum('nhd,hd->nh', h, attn_dst)
        e_score = edge_attr @ W_edge
        attn = a_src_node[src] + a_dst_node[dst] + e_score
        attn = jnp.where(attn >= 0, attn, NEG_SLOPE * attn)
        attn_max = jnp.zeros((n, H), attn.dtype).at[dst].max(attn)
        attn = jnp.exp(attn - attn_max[dst])
        attn_sum = jnp.zeros((n, H), attn.dtype).at[dst].add(attn)
        attn = attn / (attn_sum[dst] + EPS_SOFTMAX)
        msg = h[src] * attn[:, :, None]
        out = jnp.zeros((n, H, HD), h.dtype).at[dst].add(msg).reshape(n, OUT_DIM)
        y = out + h.reshape(n, OUT_DIM)
        mu = jnp.mean(y, axis=-1, keepdims=True)
        var = jnp.mean((y - mu) ** 2, axis=-1, keepdims=True)
        return (y - mu) * jax.lax.rsqrt(var + EPS_LN) * ln_gamma + ln_beta
    edge_index = jnp.stack([src, dst])
    h = jnp.maximum(_layernorm(x, axis=-1), 0.0)
    x = x + _L0_gnn_ref(h, edge_index, edge_attr_16, L0_gnn_W_node, L0_gnn_W_edge, L0_gnn_attn_src, L0_gnn_attn_dst, L0_gnn_ln_gamma, L0_gnn_ln_beta)
    return x

_drawn_inputs = setup_inputs


def setup_inputs(seed=0):
    import zlib

    import numpy as np

    out = dict(_drawn_inputs(seed))
    spreads = {'L0_gnn_ln_gamma': (1.0, 0.2), 'L0_gnn_ln_beta': (0.0, 0.1)}
    factors = {'L0_gnn_attn_dst': 13.022, 'edge_attr_16': 2.869, 'L0_gnn_W_edge': 2.807}
    for name, (base, spread) in spreads.items():
        noise = np.random.default_rng([zlib.crc32(name.encode()), seed]).standard_normal(out[name].shape)
        drawn = base * np.exp(spread * noise) if base else spread * noise
        out[name] = jnp.asarray(drawn.astype(out[name].dtype))
    for name, factor in factors.items():
        out[name] = (out[name] * factor).astype(out[name].dtype)
    return out
```

```python
import concourse.bass as bass
from concourse import mybir
from contextlib import ExitStack


OWN_CHUNK = 21


class Steps:

    def __init__(self, engine, sem):
        self.engine, self.sem, self.base, self.n = engine, sem, 0, 0

    def enter(self, step, first, per_step):
        self.before, self.per_step = self.base + self.n, per_step
        self.base, self.n = per_step * step + (self.before - per_step * first), 0

    def leave(self, turns):
        assert self.n == self.per_step, (self.n, self.per_step)
        self.base, self.n = self.before + self.per_step * turns, 0

    def link(self, instruction):
        instruction.then_inc(self.sem, 1)
        self.n += 1
        self.engine.wait_ge(self.sem, self.base + self.n)


def wait(engine, sem, value):
    if not (isinstance(value, int) and value <= 0):
        engine.wait_ge(sem, value)


class Unit:

    def __init__(self, u, kind, idx, turn, slot, ring, half=0):
        self.u, self.kind, self.idx, self.turn = u, kind, idx, turn
        self.slot, self.ring, self.half = slot, ring, half


def gnn_layer_kernel(nc, x, src, dst, edge_attr, w_node, w_edge, attn_src, attn_dst, gamma, beta, out):
    f32, i32 = mybir.dt.float32, mybir.dt.int32
    ALU, ACT, AX = mybir.AluOpType, mybir.ActivationFunctionType, mybir.AxisListType

    P = 128
    N, F = x.shape
    E, ED = edge_attr.shape
    H = w_edge.shape[1]
    HD = F // H
    EPS_LN, EPS_SOFTMAX, NEG_SLOPE = 1e-5, 1e-8, 0.2

    U = 14
    EDGES = -(-E // (P * U)) * U
    CHUNKS = EDGES // U
    LAST_E = E - (P - 1) * EDGES
    ROWS = N // P // 2 * 2
    DC = 2 * U
    REST = ROWS - (CHUNKS - 1) * DC
    TAIL = N - P * ROWS
    PT = TAIL // 2
    assert CHUNKS % 2 == 0 and 0 < LAST_E <= EDGES and U < REST and REST + 2 <= DC and TAIL % 2 == 0
    UNITS = 3 * CHUNKS
    STEPS = CHUNKS // 2
    ROWS_A = 112
    NONE = float(1 << 20)
    SCORES = U * F
    SQUARES = SCORES + U * H
    G = F + H

    ctx = ExitStack()
    with ctx:
        def sb(name, shape, dt=f32):
            return ctx.enter_context(nc.sbuf_tensor(name, shape, dt))

        def sem(name):
            return ctx.enter_context(nc.semaphore(name))

        src_rows = sb("src_rows", [P, EDGES, F])
        src_score = sb("src_score", [P, EDGES, H])
        attr = sb("attr", [P, EDGES, ED])
        src_idx = sb("src_idx", [P, EDGES], i32)
        dst_int = sb("dst_int", [P, EDGES + 2], i32)
        dst_f = sb("dst_f", [P, EDGES + 2])
        continues = sb("continues", [P, EDGES])
        head = sb("head", [P, EDGES + 1])
        head_end = sb("head_end", [P, EDGES])
        gather_idx = sb("gather_idx", [P, EDGES], i32)
        scatter_idx = sb("scatter_idx", [P, EDGES], i32)
        flag = dst_int[:, 0:EDGES].bitcast(f32)
        fix_idx = sb("fix_idx", [P, 1], i32)
        fix_f = sb("fix_f", [P, 4])
        ident = sb("ident", [P, P])
        center = sb("center", [P, P])
        w_two = sb("w_two", [P, F])
        w_pair = sb("w_pair", [P, P])
        w_pair_centered = sb("w_pair_centered", [P, P])
        w_row = sb("w_row", [P, 4])
        score_w = sb("score_w", [P, 2, 2, H])
        ones_pair = sb("ones_pair", [P, 2])
        gamma_b = sb("gamma_b", [P, F])
        beta_b = sb("beta_b", [P, F])
        wedge_b = sb("wedge_b", [P, ED, H])
        idx_now = sb("idx_now", [P, 2, U], i32)
        out_idx_now = sb("out_idx_now", [P, 2, U], i32)
        gathered = sb("gathered", [P, 2, U, F])
        nodes = sb("nodes", [P, 2 * DC * F])
        nodes_v = nodes[:, :].rearrange("p (s j f) -> p s j f", s=2, f=F)
        done_rows = sb("done_rows", [P, 2, U, F])
        xT = sb("xT", [P, 2, U * F])
        squares = sb("squares", [P, 2, U * F])
        relu = sb("relu", [P, 2, U * F])
        attn_b = relu[:, 0, 0:2 * F].rearrange("p (n f) -> p n f", n=2)
        attn_w = relu[:, 1, 0:2 * F].rearrange("p (n f) -> p n f", n=2)
        work = sb("work", [P, 2, U * F])
        var = sb("var", [P, 2, U])
        part = sb("part", [P, 2, U])
        std = sb("std", [P, 2, U])
        rstd = sb("rstd", [P, 2, U])
        dscore = sb("dscore", [P, H, U])
        escore = sb("escore", [P, H, U])
        raw = sb("raw", [P, H, U])
        score = sb("score", [P, H, U + 1])
        cont4 = sb("cont4", [P, H, U + 1])
        peak = sb("peak", [P, H, U + 1])
        args = sb("args", [P, 2, H, U])
        exps = sb("exps", [P, 2, H, U])
        decay4 = sb("decay4", [P, H, U + 1])
        inv = sb("inv", [P, H, U])
        mean = sb("mean", [P, U])
        peak_t = sb("peak_t", [P, H, U])
        head_add = sb("head_add", [P, G + H])
        head_sum = sb("head_sum", [P, G])
        head_peak = sb("head_peak", [P, H])
        R = G * (U + 1)
        decay = nodes[:, 0:R].rearrange("p (g k) -> p g k", g=G)
        terms = nodes[:, R:2 * R].rearrange("p (g k) -> p g k", g=G)
        sums = nodes[:, 2 * R:3 * R].rearrange("p (g k) -> p g k", g=G)

        psT = ctx.enter_context(nc.psum_tensor("psT", [P, 1024], f32))
        psC = ctx.enter_context(nc.psum_tensor("psC", [P, 1024], f32))
        psH = [ctx.enter_context(nc.psum_tensor(f"psH{r}", [P, 1024], f32)) for r in range(2)]

        weights_in = sem("weights_in")
        src_in = sem("src_in")
        dst_in = sem("dst_in")
        attr_in = sem("attr_in")
        nodes_in = [[sem(f"nodes_in{s}{h}") for h in range(2)] for s in range(2)]
        rows_gathered = [sem(f"rows_gathered{s}") for s in range(2)]
        rows_stored = [sem(f"rows_stored{s}") for s in range(2)]
        rows_scattered = [sem(f"rows_scattered{s}") for s in range(2)]
        pads_set = sem("pads_set")
        idx_staged = sem("idx_staged")
        out_idx_staged = sem("out_idx_staged")
        pool_const = sem("pool_const")
        const_ready = sem("const_ready")
        flags_ready = sem("flags_ready")
        turned = sem("turned")
        turned_copied = sem("turned_copied")
        centered = sem("centered")
        relu_ready = sem("relu_ready")
        h_ready = sem("h_ready")
        h_free = sem("h_free")
        h_squared = sem("h_squared")
        var_ready = sem("var_ready")
        std_ready = sem("std_ready")
        rows_done = sem("rows_done")
        args_ready = sem("args_ready")
        exps_ready = sem("exps_ready")
        decay_ready = sem("decay_ready")
        decay_long = sem("decay_long")
        y_centered = sem("y_centered")
        y_squared = sem("y_squared")
        var2_ready = sem("var2_ready")
        std2_ready = sem("std2_ready")
        final_done = sem("final_done")
        dve_steps = sem("dve_steps")
        ends_ready = sem("ends_ready")
        ends_turned = sem("ends_turned")
        fix_args = sem("fix_args")
        fix_exps = sem("fix_exps")
        fix_args2 = sem("fix_args2")
        fix_exps2 = sem("fix_exps2")
        totals_ready = sem("totals_ready")
        totals_turned = sem("totals_turned")
        fix_gathered = sem("fix_gathered")
        fix_scattered = sem("fix_scattered")

        block = ctx.enter_context(nc.Block())

        PER_GATHER = 16 * U

        def unit1(s, i):
            if isinstance(s, int) and 6 * s + i >= UNITS:
                return unit2(0, 6 * s + i - UNITS)
            it, k = divmod(i, 3)
            return Unit(s * 6 + i, "node" if k else "src", s * 2 + it, s + it // 2, it % 2, i % 2, max(k - 1, 0))

        def unit2(s, j):
            return Unit(s * 2 + (UNITS + j), "dst", s * 2 + j, s + j // 2, j % 2, j % 2)

        FIX = unit2(0, CHUNKS)

        def partition_rows(dram, width):
            return dram[0:(P - 1) * EDGES].rearrange("(p k) -> p k", p=P - 1) if width == 1 else \
                dram[0:(P - 1) * EDGES, :].rearrange("(p k) d -> p k d", p=P - 1)

        x_main = x[0:P * ROWS, :].rearrange("(p j) f -> p (j f)", j=ROWS)
        x_tail = x[P * ROWS:N, :].rearrange("(p j) f -> p (j f)", j=2)
        out_main = out[0:P * ROWS, :].rearrange("(p j) f -> p (j f)", j=ROWS)
        out_tail = out[P * ROWS:N, :].rearrange("(p j) f -> p (j f)", j=2)

        ends = relu[:, :, :].rearrange("p r c -> p (r c)")[:, 0:5 * G].rearrange("p (n g) -> p n g", n=5)
        ends_t = squares[0:G, :, :].rearrange("p r c -> p (r c)")[:, 0:5 * P].rearrange("p (n q) -> p n q", n=5)
        line = xT[0:G, :, :].rearrange("p r c -> p (r c)")[:, 0:12 * (P + 1)].rearrange("p (n q) -> p n q", n=12)
        totals = line[:, 11, 0:P]

        def ends_ps(n):
            return psT[0:G, n * P:(n + 1) * P] if n < 4 else psT[0:G, 512:512 + P]

        @block.sync
        def _(sp):
            def edge_parts(tile, dram, width, done):
                full = partition_rows(dram, width)
                sp.dma_start(tile[0:ROWS_A], full[0:ROWS_A]).then_inc(done, 16)
                sp.dma_start(tile[ROWS_A:P - 1], full[ROWS_A:P - 1]).then_inc(done, 16)
                last = dram[(P - 1) * EDGES:E] if width == 1 else dram[(P - 1) * EDGES:E, :]
                sp.dma_start(tile[P - 1:P, 0:LAST_E], last.unsqueeze(0)).then_inc(done, 16)

            def load_nodes(u):
                to = (2 * u.slot + u.half) * (U * F)
                sp.dma_start(nodes[:, to:to + U * F], x_main[:, bass.ds(u.idx * (DC * F) + u.half * (U * F), U * F)])\
                    .then_inc(nodes_in[u.slot][u.half], 16)

            sp.wait_ge(pads_set, 3)
            edge_parts(src_idx[:, :], src, 1, src_in)
            for i in (1, 2, 4, 5):
                load_nodes(unit1(0, i))
            sp.dma_start(w_two[0:F, :], w_node).then_inc(weights_in, 16)
            sp.dma_start(w_two[F:P, :], w_node).then_inc(weights_in, 16)
            for n, a in enumerate((attn_src, attn_dst)):
                sp.dma_start(attn_b[:, n, :], a.rearrange("h d -> (h d)").partition_broadcast(P)).then_inc(weights_in, 16)
            sp.dma_start(gamma_b[:, :], gamma.partition_broadcast(P)).then_inc(weights_in, 16)
            sp.dma_start(beta_b[:, :], beta.partition_broadcast(P)).then_inc(weights_in, 16)
            sp.dma_start(wedge_b[:, :, :].rearrange("p d h -> p (d h)"),
                         w_edge.rearrange("d h -> (d h)").partition_broadcast(P)).then_inc(weights_in, 16)
            edge_parts(dst_int[:, 1:EDGES + 1], dst, 1, dst_in)
            for to, at in ((dst_int[1:P, 0:1], EDGES - 1), (dst_int[0:P - 1, EDGES + 1:EDGES + 2], EDGES)):
                step = dst[at:at + (P - 2) * EDGES + 1:EDGES]
                sp.dma_start(to, step.unsqueeze(1), allow_slow_non_contiguous=True).then_inc(dst_in, 16)
            edge_parts(attr[:, :, :], edge_attr, ED, attr_in)

            def store(u):
                sp.wait_ge(rows_done, u.idx * 2 + (u.half + 1))
                sp.dma_start(out_main[:, bass.ds(u.idx * (DC * F) + u.half * (U * F), U * F)],
                             done_rows[:, u.half].rearrange("p j f -> p (j f)")).then_inc(rows_stored[u.half], 16)

            with sp.Fori(0, STEPS - 2) as s:
                for i in (1, 2, 4, 5):
                    store(unit1(s, i))
                    load_nodes(unit1(s, i + 6))
            for t in range(CHUNKS - 4, CHUNKS - 1):
                for i in (1, 2):
                    store(unit1(0, 3 * t + i))
                    if t + 2 < CHUNKS - 1:
                        load_nodes(unit1(0, 3 * (t + 2) + i))
                if t + 2 == CHUNKS - 1:
                    base, at = DC * F, (CHUNKS - 1) * DC * F
                    sp.dma_start(nodes[:, base:base + U * F], x_main[:, at:at + U * F]).then_inc(nodes_in[1][0], 16)
                    sp.dma_start(nodes[:, base + U * F:base + REST * F], x_main[:, at + U * F:ROWS * F])\
                        .then_inc(nodes_in[1][1], 16)
                    sp.dma_start(nodes[0:PT, base + REST * F:base + (REST + 2) * F], x_tail).then_inc(nodes_in[1][1], 16)
            at, left = (CHUNKS - 1) * DC * F, REST - U
            store(unit1(0, UNITS - 2))
            sp.wait_ge(rows_done, 2 * CHUNKS)
            sp.dma_start(out_main[:, at + U * F:ROWS * F],
                         done_rows[:, 1, 0:left, :].rearrange("p j f -> p (j f)")).then_inc(rows_stored[1], 16)
            sp.dma_start(out_tail, done_rows[0:PT, 1, left:left + 2, :].rearrange("p j f -> p (j f)"))\
                .then_inc(rows_stored[1], 16)
            for half in range(2):
                sp.wait_ge(rows_stored[half], 16 * (CHUNKS + half))

        @block.gpsimd
        def _(pool):
            def gather(idx, u):
                nc.gpsimd.tensor_copy(idx_now[:, u.slot, :], idx[:, bass.ds(u.idx * U, U)]).then_inc(idx_staged, 1)
                pool.wait_ge(idx_staged, 1)
                pool.sem_clear(idx_staged)
                for k in range(U):
                    nc.gpsimd.indirect_dma_start(
                        out=gathered[:, u.slot, k, :], out_offset=None, in_=x[:, :],
                        in_offset=bass.IndirectOffsetOnAxis(ap=idx_now[:, u.slot, k:k + 1], axis=0),
                        bounds_check=N - 1, oob_is_err=False).then_inc(rows_gathered[u.slot], 16)

            def scatter(u):
                pool.wait_ge(final_done, u.idx + 1)
                nc.gpsimd.tensor_copy(out_idx_now[:, u.slot, :],
                                      scatter_idx[:, bass.ds(u.idx * U, U)]).then_inc(out_idx_staged, 1)
                pool.wait_ge(out_idx_staged, 1)
                pool.sem_clear(out_idx_staged)
                for k in range(U):
                    nc.gpsimd.indirect_dma_start(
                        out=out[:, :],
                        out_offset=bass.IndirectOffsetOnAxis(ap=out_idx_now[:, u.slot, k:k + 1], axis=0),
                        in_=done_rows[:, u.slot, k, :], in_offset=None,
                        bounds_check=N - 1, oob_is_err=False).then_inc(rows_scattered[u.slot], 16)

            pool.wait_ge(src_in, 48)
            gather(src_idx, unit1(0, 0))
            nc.gpsimd.memset(ident[:, :], 0.0).then_inc(pool_const, 1)
            pool.wait_ge(pool_const, 1)
            nc.gpsimd.affine_select(out=ident[:, :], in_=ident[:, :], compare_op=ALU.not_equal, fill=1.0, base=0,
                                    pattern=[[-1, P]], channel_multiplier=1).then_inc(pool_const, 1)
            gather(src_idx, unit1(0, 3))
            with pool.Fori(0, STEPS - 1) as s:
                for i in (6, 9):
                    u = unit1(s, i)
                    pool.wait_ge(turned, u.u - 5)
                    pool.wait_ge(rows_gathered[u.slot], PER_GATHER * u.turn)
                    gather(src_idx, u)
            pool.wait_ge(flags_ready, 1)
            for j in range(2):
                u = unit2(0, j)
                pool.wait_ge(turned, UNITS - 5 + 3 * j)
                pool.wait_ge(rows_gathered[u.slot], PER_GATHER * STEPS)
                gather(gather_idx, u)
            for half in range(2):
                pool.wait_ge(rows_stored[half], 16 * (CHUNKS + half))

            def gather_and_scatter(before, u):
                pool.wait_ge(final_done, before.idx + 1)
                pool.wait_ge(rows_gathered[u.slot], PER_GATHER * (u.turn + STEPS))
                gather(gather_idx, u)
                wait(pool, rows_scattered[u.slot], PER_GATHER * before.turn)
                scatter(before)

            for j in range(2):
                gather_and_scatter(unit2(0, j), unit2(0, j + 2))
            with pool.Fori(1, STEPS - 1) as s:
                for j in range(2):
                    gather_and_scatter(unit2(s, j), unit2(s, j + 2))
            for j in range(CHUNKS - 2, CHUNKS):
                u = unit2(0, j)
                pool.wait_ge(rows_scattered[u.slot], PER_GATHER * u.turn)
                scatter(u)
            pool.wait_ge(final_done, CHUNKS - 1)
            nc.gpsimd.indirect_dma_start(
                out=gathered[:, FIX.slot, 0, :], out_offset=None, in_=x[:, :],
                in_offset=bass.IndirectOffsetOnAxis(ap=gather_idx[:, 0:1], axis=0),
                bounds_check=N - 1, oob_is_err=False).then_inc(fix_gathered, 16)
            pool.wait_ge(final_done, CHUNKS + 1)
            nc.gpsimd.indirect_dma_start(
                out=out[:, :], out_offset=bass.IndirectOffsetOnAxis(ap=fix_idx[:, 0:1], axis=0),
                in_=done_rows[:, FIX.slot, 0, :], in_offset=None,
                bounds_check=N - 1, oob_is_err=False).then_inc(fix_scattered, 16)
            for slot in range(2):
                pool.wait_ge(rows_scattered[slot], PER_GATHER * STEPS)
            pool.wait_ge(fix_scattered, 16)

        @block.tensor
        def _(pe):
            def turn(u):
                if u.kind == "src":
                    pe.wait_ge(rows_gathered[u.slot], PER_GATHER * (u.turn + 1))
                elif u is FIX:
                    pe.wait_ge(fix_gathered, 16)
                elif u.kind == "dst":
                    pe.wait_ge(rows_gathered[u.slot], PER_GATHER * (u.turn + 1 + STEPS))
                else:
                    last = isinstance(u.idx, int) and u.u == UNITS - 1
                    pe.wait_ge(nodes_in[u.slot][u.half], 16 * (u.turn + 1 + last))
                pe.wait_ge(turned_copied, u.u)
                rows = gathered[:, u.slot] if u.kind != "node" else \
                    nodes_v[:, u.slot, u.half * U:(u.half + 1) * U, :]
                for m in range(U // 2):
                    last = nc.tensor.transpose(psT[:, m * P:(m + 1) * P],
                                               rows[:, 2 * m:2 * m + 2, :].rearrange("p j f -> p (j f)"), ident[:, :])
                last.then_inc(turned, 1)

            def take_mean(u):
                pe.wait_ge(turned_copied, u.u + 1)
                pe.wait_ge(relu_ready, u.u)
                for a in range(0, U * F, 512):
                    b = min(a + 512, U * F)
                    last = nc.tensor.matmul(psC[:, a:b], center[:, :], xT[:, u.ring, a:b], start=True, stop=True)
                last.then_inc(centered, 1)

            def project(u):
                pe.wait_ge(relu_ready, u.u + 1)
                pe.wait_ge(h_free, u.u + 1)
                w = w_pair_centered if u.kind == "node" else w_pair
                for m in range(U // 2):
                    rows = relu[:, u.ring, m * P:(m + 1) * P]
                    nc.tensor.matmul(psH[u.ring][:, m * P:(m + 1) * P], rows, w[:, :], start=True, stop=True)
                    if u.kind != "node":
                        nc.tensor.matmul(psH[u.ring][:, SCORES + 2 * H * m:SCORES + 2 * H * (m + 1)], rows,
                                         score_w[:, int(u.kind == "dst")].rearrange("p r h -> p (r h)"),
                                         start=True, stop=True)
                    last = nc.tensor.matmul(psH[u.ring][:, SQUARES + 2 * m:SQUARES + 2 * (m + 1)],
                                            squares[:, u.ring, m * P:(m + 1) * P], ones_pair[:, :],
                                            start=True, stop=True)
                last.then_inc(h_ready, 1)

            pe.sem_inc(h_free, 2)
            pe.wait_ge(pool_const, 2)
            turn(unit1(0, 0))
            turn(unit1(0, 1))
            pe.wait_ge(const_ready, 1)
            take_mean(unit1(0, 0))
            with pe.Fori(0, STEPS - 1) as s:
                for i in range(6):
                    turn(unit1(s, i + 2))
                    take_mean(unit1(s, i + 1))
                    project(unit1(s, i))
            for i in range(6):
                if i < 4:
                    turn(unit1(STEPS - 1, i + 2))
                if i < 5:
                    take_mean(unit1(STEPS - 1, i + 1))
                project(unit1(STEPS - 1, i))
            with pe.Fori(0, STEPS) as s:
                for j in range(2):
                    turn(unit2(s, j))
                    take_mean(unit2(s, j))
                    project(unit2(s, j))
            turn(FIX)
            take_mean(FIX)
            project(FIX)
            pe.wait_ge(ends_ready, 1)
            for n in range(5):
                last = nc.tensor.transpose(ends_ps(n), ends[:, n, :], ident[:, :])
            last.then_inc(ends_turned, 1)
            pe.wait_ge(totals_ready, 1)
            nc.tensor.transpose(psC[:, 0:G], totals[:, :], ident[0:G, 0:G]).then_inc(totals_turned, 1)

        @block.scalar
        def _(act):
            def copy_turned(u):
                act.wait_ge(turned, u.u + 1)
                nc.scalar.copy(xT[:, u.ring, :], psT[:, 0:U * F]).then_inc(turned_copied, 1)

            def square_and_relu(u):
                act.wait_ge(centered, u.u + 1)
                nc.scalar.square(squares[:, u.ring, :], psC[:, 0:U * F])
                nc.scalar.activation(relu[:, u.ring, :], psC[:, 0:U * F], ACT.Relu).then_inc(relu_ready, 1)

            def square_h(u):
                act.wait_ge(h_ready, u.u + 1)
                if u.kind == "node":
                    nc.scalar.square(work[:, u.ring, :], psH[u.ring][:, 0:U * F]).then_inc(h_squared, 1)

            def root(u):
                act.wait_ge(var_ready, u.u + 1)
                nc.scalar.sqrt(std[:, u.ring, :], var[:, u.ring, :]).then_inc(std_ready, 1)

            def step(s, i):
                root(unit1(s, i - 2))
                copy_turned(unit1(s, i + 1))
                square_and_relu(unit1(s, i))
                square_h(unit1(s, i - 1))

            copy_turned(unit1(0, 0))
            copy_turned(unit1(0, 1))
            square_and_relu(unit1(0, 0))
            copy_turned(unit1(0, 2))
            square_and_relu(unit1(0, 1))
            square_h(unit1(0, 0))
            with act.Fori(0, STEPS - 1) as s:
                for i in range(2, 8):
                    step(s, i)
            for i in range(2, 5):
                step(STEPS - 1, i)
            root(unit1(STEPS - 1, 3))
            square_and_relu(unit1(STEPS - 1, 5))
            square_h(unit1(STEPS - 1, 4))
            root(unit1(STEPS - 1, 4))
            square_h(unit1(STEPS - 1, 5))
            root(unit1(STEPS - 1, 5))

            def front(u):
                copy_turned(u)
                square_and_relu(u)
                root(u)

            def final(n):
                act.wait_ge(y_centered, n)
                y = done_rows[:, 0 if isinstance(n, int) else slot_of[0], :, :]
                nc.scalar.square(work[:, 1, :], y.rearrange("p j f -> p (j f)")).then_inc(y_squared, 1)
                act.wait_ge(var2_ready, n)
                nc.scalar.sqrt(std[:, 1, :], var[:, 1, :]).then_inc(std2_ready, 1)

            slot_of = [0]
            with act.Fori(0, STEPS) as s:
                for j in range(2):
                    u = unit2(s, j)
                    slot_of[0] = u.slot
                    front(u)
                    act.wait_ge(args_ready, u.idx + 1)
                    nc.scalar.activation(exps[:, :, :, :], args[:, :, :, :], ACT.Exp).then_inc(exps_ready, 1)
                    act.wait_ge(decay_ready, u.idx + 1)
                    for h in range(H):
                        nc.scalar.copy(decay[:, h * HD:(h + 1) * HD, :],
                                       decay4[:, h, :].unsqueeze(1).broadcast_to([P, HD, U + 1]))
                    nc.scalar.copy(decay[:, F:G, :], decay4[:, :, :]).then_inc(decay_long, 1)
                    final(u.idx + 1)
            front(FIX)
            act.wait_ge(ends_turned, 1)
            nc.scalar.copy(ends_t[:, 0:4, :].rearrange("p n q -> p (n q)"), psT[0:G, 0:512])
            nc.scalar.copy(ends_t[:, 4, :], psT[0:G, 512:512 + P]).then_inc(ends_turned, 1)
            act.wait_ge(fix_args, 1)
            nc.scalar.activation(line[:, 4:6, 0:P], line[:, 2:4, 0:P], ACT.Exp).then_inc(fix_exps, 1)
            act.wait_ge(fix_args2, 1)
            nc.scalar.activation(line[:, 4:6, 0:P], line[:, 2:4, 0:P], ACT.Exp).then_inc(fix_exps2, 1)
            final(CHUNKS + 1)

        @block.vector
        def _(dve):
            V = nc.vector
            own = Steps(dve, dve_steps)
            link = own.link

            V.memset(src_idx[96:P, :], 0).then_inc(pads_set, 1)
            V.memset(dst_int[:, :], int(NONE)).then_inc(pads_set, 1)
            V.memset(attr[96:P, LAST_E:, :], 0.0).then_inc(pads_set, 1)
            V.memset(center[:, :], 0.0)
            V.memset(w_pair[:, :], 0.0)
            V.memset(w_pair_centered[:, :], 0.0)
            V.memset(score_w[:, :, :, :], 0.0)
            link(V.memset(ones_pair[:, :], 0.0))
            for r in range(2):
                lo = r * F
                V.memset(center[lo:lo + F, lo:lo + F], -1.0 / F)
                link(V.memset(ones_pair[lo:lo + F, r:r + 1], 1.0))
            dve.wait_ge(pool_const, 2)
            V.tensor_tensor(center[:, :], center[:, :], ident[:, :], ALU.add)
            dve.wait_ge(weights_in, 7 * 16)
            link(V.tensor_reduce(w_row[:, 0:1], w_two[:, :], AX.X, ALU.add))
            V.tensor_scalar(w_row[:, 1:2], w_row[:, 0:1], 1.0 / F, None, ALU.mult)
            for n in range(2):
                V.tensor_tensor(attn_w[:, n, :], w_two[:, :], attn_b[:, n, :], ALU.mult)
            link(V.memset(w_row[:, 2:3], 0.0))
            for r in range(2):
                lo = r * F
                V.tensor_copy(w_pair[lo:lo + F, lo:lo + F], w_two[lo:lo + F, :])
                V.tensor_scalar(w_pair_centered[lo:lo + F, lo:lo + F], w_two[lo:lo + F, :],
                                w_row[lo:lo + F, 1:2], None, ALU.subtract)
                for n in range(2):
                    last = V.tensor_reduce(score_w[lo:lo + F, n, r, :],
                                           attn_w[lo:lo + F, n, :].rearrange("p (h d) -> p h d", h=H), AX.X, ALU.add)
            last.then_inc(const_ready, 1)

            dve.wait_ge(dst_in, 5 * 16)
            link(V.tensor_copy(dst_f[:, :], dst_int[:, :]))
            link(V.memset(dst_f[0:1, 0:1], -1.0))
            here, prev, nxt = dst_f[:, 1:EDGES + 1], dst_f[:, 0:EDGES], dst_f[:, 2:EDGES + 2]
            V.tensor_tensor(continues[:, :], here, prev, ALU.is_equal)
            V.tensor_scalar(head[:, 0:EDGES], here, dst_f[:, 0:1], None, ALU.is_equal)
            V.tensor_scalar(gather_idx[:, :], here, float(N - 1), None, ALU.min)
            link(V.tensor_tensor(flag, here, nxt, ALU.not_equal))
            V.memset(continues[:, 0:1], 0.0)
            link(V.memset(head[:, EDGES:EDGES + 1], 0.0))
            V.tensor_tensor(head_end[:, :], head[:, 0:EDGES], head[:, 1:EDGES + 1], ALU.subtract)
            link(V.tensor_tensor(flag, flag, head[:, 0:EDGES], ALU.is_gt))
            link(V.scalar_tensor_tensor(flag, here, NONE, flag, ALU.subtract, ALU.mult))
            V.tensor_scalar(scatter_idx[:, :], flag, NONE, None, ALU.add)
            link(V.tensor_tensor(fix_f[:, 0:1], here[:, EDGES - 1:EDGES], nxt[:, EDGES - 1:EDGES], ALU.is_equal))
            link(V.tensor_tensor(fix_f[:, 1:2], fix_f[:, 0:1], head[:, EDGES - 1:EDGES], ALU.mult))
            link(V.tensor_tensor(fix_f[:, 2:3], head[:, 0:1], fix_f[:, 1:2], ALU.is_gt))
            link(V.scalar_tensor_tensor(fix_f[:, 3:4], here[:, 0:1], NONE, fix_f[:, 2:3], ALU.subtract, ALU.mult))
            V.tensor_scalar(fix_idx[:, :], fix_f[:, 3:4], NONE, None, ALU.add).then_inc(flags_ready, 1)

            def variances(u):
                dve.wait_ge(h_ready, u.u + 1)
                sq = psH[u.ring][:, SQUARES:SQUARES + U]
                if u.kind != "node":
                    V.tensor_scalar(var[:, u.ring, :], sq, 1.0 / F, EPS_LN, ALU.mult, ALU.add).then_inc(var_ready, 1)
                    return
                dve.wait_ge(h_squared, u.idx * 2 + (u.half + 1))
                V.tensor_scalar(part[:, 0, :], sq, EPS_LN / F, EPS_LN * EPS_LN, ALU.mult, ALU.add)
                link(V.tensor_reduce(part[:, 1, :], work[:, u.ring, :].rearrange("p (j f) -> p j f", f=F), AX.X, ALU.add))
                V.scalar_tensor_tensor(var[:, u.ring, :], part[:, 1, :], 1.0 / F, part[:, 0, :],
                                       ALU.mult, ALU.add).then_inc(var_ready, 1)

            def wide(ap, n=F):
                return ap.unsqueeze(2).broadcast_to([P, U, n])

            def every(ap):
                return ap.unsqueeze(1).broadcast_to([P, U, F])

            def h_of(u):
                return psH[u.ring][:, 0:U * F].rearrange("p (j f) -> p j f", f=F)

            def scores_of(u):
                return psH[u.ring][:, SCORES:SQUARES].rearrange("p (j h) -> p j h", h=H)

            def scale(u):
                dve.wait_ge(std_ready, u.u + 1)
                link(V.reciprocal(rstd[:, u.ring, :], std[:, u.ring, :]))
                if u.kind == "src":
                    at = bass.ds(u.idx * U, U)
                    V.tensor_tensor(src_score[:, at, :], scores_of(u), wide(rstd[:, u.ring, :], H), ALU.mult)
                    V.tensor_tensor(src_rows[:, at, :], h_of(u), wide(rstd[:, u.ring, :]), ALU.mult).then_inc(h_free, 1)
                    return
                wait(dve, rows_stored[u.half], 16 * u.idx)
                V.tensor_tensor(done_rows[:, u.half], h_of(u), wide(rstd[:, u.ring, :]), ALU.mult).then_inc(h_free, 1)

            def add_residual(u):
                if u.kind == "src":
                    return
                y = done_rows[:, u.half]
                x_rows = nodes_v[:, u.slot, u.half * U:(u.half + 1) * U, :]
                dve.wait_ge(h_free, u.u + 3)
                link(V.tensor_tensor(y, y, every(gamma_b[:, :]), ALU.mult))
                link(V.tensor_tensor(y, y, every(beta_b[:, :]), ALU.add))
                V.tensor_tensor(y, y, x_rows, ALU.add).then_inc(rows_done, 1)

            def step(s, i):
                variances(unit1(s, i))
                add_residual(unit1(s, i - 1))
                scale(unit1(s, i))

            variances(unit1(0, 0))
            scale(unit1(0, 0))
            for i in range(1, 7):
                step(0, i)
            with dve.Fori(1, STEPS - 1) as s:
                own.enter(s, 1, 6 + 4 * 3)
                for i in range(1, 7):
                    step(s, i)
                own.leave(STEPS - 2)
            for i in range(1, 6):
                step(STEPS - 1, i)
            add_residual(unit1(STEPS - 1, 5))

            dve.wait_ge(attr_in, 48)
            for half in range(2):
                dve.wait_ge(rows_stored[half], 16 * (CHUNKS + half))
            V.memset(sums, 0.0)
            V.memset(peak[:, :, :], 0.0)
            V.memset(cont4[:, :, :], 0.0)
            V.memset(decay4[:, :, :], 0.0)
            V.memset(head_sum[:, :], 0.0)
            link(V.memset(head_peak[:, :], 0.0))

            def heads(ap):
                return ap.unsqueeze(2).broadcast_to([P, H, HD, U])

            def output(u, n):
                y = done_rows[:, u.slot, :, :]
                agg = work[:, 0, :].rearrange("p (j f) -> p j f", f=F)
                if u is not FIX:
                    wait(dve, rows_scattered[u.slot], PER_GATHER * u.turn)
                else:
                    dve.wait_ge(rows_scattered[u.slot], PER_GATHER * STEPS)
                V.tensor_tensor(y, h_of(u), wide(rstd[:, 0, :]), ALU.mult).then_inc(h_free, 1)
                dve.wait_ge(h_free, u.u + 3)
                link(V.tensor_tensor(y, y, agg, ALU.add))
                link(V.tensor_reduce(mean[:, :], y, AX.X, ALU.add))
                link(V.tensor_scalar(mean[:, :], mean[:, :], 1.0 / F, None, ALU.mult))
                V.tensor_tensor(y, y, wide(mean[:, :]), ALU.subtract).then_inc(y_centered, 1)
                dve.wait_ge(y_squared, n)
                link(V.tensor_reduce(part[:, 1, :], work[:, 1, :].rearrange("p (j f) -> p j f", f=F), AX.X, ALU.add))
                V.tensor_scalar(var[:, 1, :], part[:, 1, :], 1.0 / F, EPS_LN, ALU.mult, ALU.add).then_inc(var2_ready, 1)
                dve.wait_ge(std2_ready, n)
                link(V.reciprocal(rstd[:, 1, :], std[:, 1, :]))
                link(V.tensor_tensor(y, y, wide(rstd[:, 1, :]), ALU.mult))
                link(V.tensor_tensor(y, y, every(gamma_b[:, :]), ALU.mult))
                link(V.tensor_tensor(y, y, every(beta_b[:, :]), ALU.add))
                V.tensor_tensor(y, y, gathered[:, u.slot, :, :], ALU.add).then_inc(final_done, 1)

            def chunk(u):
                at = bass.ds(u.idx * U, U)
                tmp = work[:, 1, :].rearrange("p (k h d) -> p k h d", h=H, d=ED)
                V.tensor_copy(score[:, :, 0:1], peak[:, :, U:U + 1])
                V.tensor_copy(terms[:, :, 0:1], sums[:, :, U:U + 1])
                V.tensor_copy(cont4[:, :, 1:U + 1], continues[:, at].unsqueeze(1).broadcast_to([P, H, U]))
                link(V.tensor_tensor(tmp, attr[:, at, :].unsqueeze(2).broadcast_to([P, U, H, ED]),
                                     wedge_b[:, :, :].rearrange("p d h -> p h d").unsqueeze(1)
                                     .broadcast_to([P, U, H, ED]), ALU.mult))
                link(V.tensor_reduce(escore[:, :, :].rearrange("p h k -> p k h"), tmp, AX.X, ALU.add))
                V.tensor_tensor(raw[:, :, :], src_score[:, at, :].rearrange("p k h -> p h k"), escore[:, :, :], ALU.add)
                variances(u)
                dve.wait_ge(std_ready, u.u + 1)
                link(V.reciprocal(rstd[:, 0, :], std[:, u.ring, :]))
                link(V.tensor_tensor(dscore[:, :, :], scores_of(u).rearrange("p j h -> p h j"),
                                     rstd[:, 0, :].unsqueeze(1).broadcast_to([P, H, U]), ALU.mult))
                link(V.tensor_tensor(raw[:, :, :], raw[:, :, :], dscore[:, :, :], ALU.add))
                link(V.scalar_tensor_tensor(score[:, :, 1:U + 1], raw[:, :, :], NEG_SLOPE, raw[:, :, :],
                                            ALU.mult, ALU.max))
                link(V.tensor_tensor_scan(peak[:, :, :].rearrange("p h k -> p (h k)"),
                                          cont4[:, :, :].rearrange("p h k -> p (h k)"),
                                          score[:, :, :].rearrange("p h k -> p (h k)"), 0.0, ALU.mult, ALU.max))
                V.tensor_tensor(args[:, 0], score[:, :, 1:U + 1], peak[:, :, 1:U + 1], ALU.subtract)
                link(V.tensor_tensor(args[:, 1], peak[:, :, 0:U], peak[:, :, 1:U + 1], ALU.subtract))
                V.tensor_scalar(args[:, 1], args[:, 1], 0.0, None, ALU.min).then_inc(args_ready, 1)
                dve.wait_ge(exps_ready, u.idx + 1)
                V.tensor_tensor(decay4[:, :, 1:U + 1], exps[:, 1], cont4[:, :, 1:U + 1], ALU.mult).then_inc(decay_ready, 1)
                V.tensor_copy(terms[:, F:G, 1:U + 1], exps[:, 0])
                for h in range(H):
                    last = V.tensor_tensor(terms[:, h * HD:(h + 1) * HD, 1:U + 1],
                                           src_rows[:, at, h * HD:(h + 1) * HD].rearrange("p k d -> p d k"),
                                           exps[:, 0, h, :].unsqueeze(1).broadcast_to([P, HD, U]), ALU.mult)
                link(last)
                dve.wait_ge(decay_long, u.idx + 1)
                link(V.tensor_tensor_scan(sums.rearrange("p g k -> p (g k)"), decay.rearrange("p g k -> p (g k)"),
                                          terms.rearrange("p g k -> p (g k)"), 0.0, ALU.mult, ALU.add))
                V.tensor_tensor(decay[:, :, 0:U], sums[:, :, 1:U + 1],
                                head_end[:, at].unsqueeze(1).broadcast_to([P, G, U]), ALU.mult)
                V.tensor_tensor(peak_t[:, :, :], peak[:, :, 1:U + 1],
                                head_end[:, at].unsqueeze(1).broadcast_to([P, H, U]), ALU.mult)
                link(V.tensor_scalar(inv[:, :, :], sums[:, F:G, 1:U + 1], EPS_SOFTMAX, None, ALU.add))
                V.tensor_reduce(head_add[:, 0:G], decay[:, :, 0:U], AX.X, ALU.add)
                V.tensor_reduce(head_add[:, G:G + H], peak_t[:, :, :], AX.X, ALU.add)
                link(V.reciprocal(inv[:, :, :], inv[:, :, :]))
                V.tensor_tensor(head_sum[:, :], head_sum[:, :], head_add[:, 0:G], ALU.add)
                V.tensor_tensor(head_peak[:, :], head_peak[:, :], head_add[:, G:G + H], ALU.add)
                agg = work[:, 0, :].rearrange("p (j f) -> p f j", f=F)
                for h in range(H):
                    last = V.tensor_tensor(agg[:, h * HD:(h + 1) * HD, :], sums[:, h * HD:(h + 1) * HD, 1:U + 1],
                                           inv[:, h, :].unsqueeze(1).broadcast_to([P, HD, U]), ALU.mult)
                link(last)
                output(u, u.idx + 1)

            for j in range(2):
                chunk(unit2(0, j))
            with dve.Fori(1, STEPS) as s:
                own.enter(s, 1, 2 * OWN_CHUNK)
                for j in range(2):
                    chunk(unit2(s, j))
                own.leave(STEPS - 1)

            u = FIX
            variances(u)
            for h in range(H):
                f0, f1 = h * HD, (h + 1) * HD
                V.tensor_copy(ends[:, 0, f0:f1], peak[:, h, U:U + 1].broadcast_to([P, HD]))
                V.tensor_copy(ends[:, 1, f0:f1], head_peak[:, h:h + 1].broadcast_to([P, HD]))
            V.tensor_copy(ends[:, 0, F:G], peak[:, :, U])
            V.tensor_copy(ends[:, 1, F:G], head_peak[:, :])
            V.tensor_copy(ends[:, 2, :], sums[:, :, U])
            V.tensor_copy(ends[:, 3, :], head_sum[:, :])
            V.tensor_copy(ends[:, 4, :], head[:, EDGES - 1:EDGES].broadcast_to([P, G])).then_inc(ends_ready, 1)
            dve.wait_ge(std_ready, u.u + 1)
            link(V.reciprocal(rstd[:, 0, :], std[:, u.ring, :]))
            dve.wait_ge(ends_turned, 2)
            last_peak, head_peak_t, last_sum, head_sum_t, whole = (ends_t[:, n, :] for n in range(5))
            V.memset(line[:, 0:2, 0:1], 0.0)
            link(V.tensor_tensor_scan(line[:, 0, 1:P + 1], whole, last_peak, 0.0, ALU.mult, ALU.max))
            V.tensor_tensor(line[:, 2, 0:P], line[:, 0, 0:P], line[:, 0, 1:P + 1], ALU.subtract)
            link(V.tensor_tensor(line[:, 3, 0:P], last_peak, line[:, 0, 1:P + 1], ALU.subtract))
            V.tensor_scalar(line[:, 2:4, 0:P], line[:, 2:4, 0:P], 0.0, None, ALU.min).then_inc(fix_args, 1)
            dve.wait_ge(fix_exps, 1)
            V.tensor_tensor(line[:, 6, 0:P], line[:, 4, 0:P], whole, ALU.mult)
            link(V.tensor_tensor(line[:, 7, 0:P], line[:, 5, 0:P], last_sum, ALU.mult))
            link(V.tensor_tensor_scan(line[:, 1, 1:P + 1], line[:, 6, 0:P], line[:, 7, 0:P], 0.0, ALU.mult, ALU.add))
            link(V.tensor_tensor(line[:, 8, 0:P], line[:, 0, 0:P], head_peak_t, ALU.max))
            V.tensor_tensor(line[:, 2, 0:P], line[:, 0, 0:P], line[:, 8, 0:P], ALU.subtract)
            V.tensor_tensor(line[:, 3, 0:P], head_peak_t, line[:, 8, 0:P], ALU.subtract).then_inc(fix_args2, 1)
            dve.wait_ge(fix_exps2, 1)
            V.tensor_tensor(line[:, 9, 0:P], line[:, 4, 0:P], line[:, 1, 0:P], ALU.mult)
            link(V.tensor_tensor(line[:, 10, 0:P], line[:, 5, 0:P], head_sum_t, ALU.mult))
            V.tensor_tensor(totals, line[:, 9, 0:P], line[:, 10, 0:P], ALU.add).then_inc(totals_ready, 1)
            dve.wait_ge(totals_turned, 1)
            link(V.tensor_scalar(inv[:, :, 0], psC[:, F:G], EPS_SOFTMAX, None, ALU.add))
            link(V.reciprocal(inv[:, :, 0], inv[:, :, 0]))
            link(V.tensor_tensor(work[:, 0, 0:F].rearrange("p (h d) -> p h d", h=H),
                                 psC[:, 0:F].rearrange("p (h d) -> p h d", h=H),
                                 inv[:, :, 0:1].broadcast_to([P, H, HD]), ALU.mult))
            output(u, CHUNKS + 1)


_INS = ['x', 'src', 'dst', 'edge_attr_16', 'L0_gnn_W_node', 'L0_gnn_W_edge', 'L0_gnn_attn_src',
        'L0_gnn_attn_dst', 'L0_gnn_ln_gamma', 'L0_gnn_ln_beta']


def kernel(**inputs):
    import numpy as _np
    import concourse.bacc as _bacc
    from concourse import mybir as _mybir
    from concourse.bass_utils import run_bass_kernel_spmd as _run

    nc = _bacc.Bacc("TRN2", target_bir_lowering=False, num_devices=1)
    arrays, args = {}, []
    for name in _INS:
        a = _np.ascontiguousarray(inputs[name])
        arrays[f"in_{name}_dram"] = a
        args.append(nc.dram_tensor(f"in_{name}_dram", a.shape, _mybir.dt.from_np(a.dtype), kind="ExternalInput").ap())
    out = nc.dram_tensor("out_0_dram", inputs["x"].shape, _mybir.dt.float32, kind="ExternalOutput").ap()
    gnn_layer_kernel(nc, *args, out)
    r = _run(nc, [arrays], core_ids=[0])
    return r.results[0]["out_0_dram"]
```

```python
import concourse.bass as bass
from concourse import mybir
from contextlib import ExitStack


OWN_CHUNK = 21


class Steps:

    def __init__(self, engine, sem):
        self.engine, self.sem, self.base, self.n = engine, sem, 0, 0

    def enter(self, step, first, per_step):
        self.before, self.per_step = self.base + self.n, per_step
        self.base, self.n = per_step * step + (self.before - per_step * first), 0

    def leave(self, turns):
        assert self.n == self.per_step, (self.n, self.per_step)
        self.base, self.n = self.before + self.per_step * turns, 0

    def link(self, instruction):
        instruction.then_inc(self.sem, 1)
        self.n += 1
        self.engine.wait_ge(self.sem, self.base + self.n)


def wait(engine, sem, value):
    if not (isinstance(value, int) and value <= 0):
        engine.wait_ge(sem, value)


class Unit:

    def __init__(self, u, kind, idx, turn, slot, ring, half=0):
        self.u, self.kind, self.idx, self.turn = u, kind, idx, turn
        self.slot, self.ring, self.half = slot, ring, half


def gnn_layer_kernel(nc, x, src, dst, edge_attr, w_node, w_edge, attn_src, attn_dst, gamma, beta, out):
    f32, i32 = mybir.dt.float32, mybir.dt.int32
    ALU, ACT, AX = mybir.AluOpType, mybir.ActivationFunctionType, mybir.AxisListType

    P = 128
    N, F = x.shape
    E, ED = edge_attr.shape
    H = w_edge.shape[1]
    HD = F // H
    EPS_LN, EPS_SOFTMAX, NEG_SLOPE = 1e-5, 1e-8, 0.2

    U = 14
    EDGES = -(-E // (P * U)) * U
    CHUNKS = EDGES // U
    LAST_E = E - (P - 1) * EDGES
    ROWS = N // P // 2 * 2
    DC = 2 * U
    REST = ROWS - (CHUNKS - 1) * DC
    TAIL = N - P * ROWS
    PT = TAIL // 2
    assert CHUNKS % 2 == 0 and 0 < LAST_E <= EDGES and U < REST and REST + 2 <= DC and TAIL % 2 == 0
    UNITS = 3 * CHUNKS
    STEPS = CHUNKS // 2
    ROWS_A = 112
    NONE = float(1 << 20)
    G = F + H
    BANK = 512
    UH = U // 2
    SQUARES = BANK + UH * G
    assert U * F <= SQUARES and SQUARES + U <= 2 * BANK and UH * G <= BANK and UH % 2 == 1

    ctx = ExitStack()
    with ctx:
        def sb(name, shape, dt=f32):
            return ctx.enter_context(nc.sbuf_tensor(name, shape, dt))

        def sem(name):
            return ctx.enter_context(nc.semaphore(name))

        src_rows = sb("src_rows", [P, EDGES, F])
        src_score = sb("src_score", [P, EDGES, H])
        attr = sb("attr", [P, EDGES, ED])
        src_idx = sb("src_idx", [P, EDGES], i32)
        dst_int = sb("dst_int", [P, EDGES + 2], i32)
        dst_f = sb("dst_f", [P, EDGES + 2])
        continues = sb("continues", [P, EDGES])
        head = sb("head", [P, EDGES + 1])
        head_end = sb("head_end", [P, EDGES])
        gather_idx = sb("gather_idx", [P, EDGES], i32)
        scatter_idx = sb("scatter_idx", [P, EDGES], i32)
        flag = dst_int[:, 0:EDGES].bitcast(f32)
        fix_idx = sb("fix_idx", [P, 1], i32)
        fix_f = sb("fix_f", [P, 4])
        ident = sb("ident", [P, P])
        center = sb("center", [P, P])
        w_two = sb("w_two", [P, F])
        w_pair_centered = sb("w_pair_centered", [P, P])
        w_row = sb("w_row", [P, 4])
        w_pair_edge = sb("w_pair_edge", [P, 2, 2, G])
        first_h = sb("first_h", [P, F])
        first_x = sb("first_x", [P, F])
        fix_row = sb("fix_row", [P, F])
        fix_tmp = sb("fix_tmp", [P, F])
        fix_stat = sb("fix_stat", [P, 8])
        ones_pair = sb("ones_pair", [P, 2])
        gamma_b = sb("gamma_b", [P, F])
        beta_b = sb("beta_b", [P, F])
        wedge_b = sb("wedge_b", [P, ED, H])
        idx_now = sb("idx_now", [P, 2, U], i32)
        out_idx_now = sb("out_idx_now", [P, 2, U], i32)
        gathered = sb("gathered", [P, 2, U, F])
        nodes = sb("nodes", [P, 2 * DC * F])
        nodes_v = nodes[:, :].rearrange("p (s j f) -> p s j f", s=2, f=F)
        done_rows = sb("done_rows", [P, 2, U, F])
        xT = sb("xT", [P, 2, U * F])
        squares = sb("squares", [P, 2, U * F])
        relu = sb("relu", [P, 2, U * F])
        attn_b = relu[:, 0, 0:2 * F].rearrange("p (n f) -> p n f", n=2)
        attn_w = relu[:, 1, 0:2 * F].rearrange("p (n f) -> p n f", n=2)
        work = sb("work", [P, 2, U * F])
        var = sb("var", [P, 2, U])
        part = sb("part", [P, 2, U])
        std = sb("std", [P, 2, U])
        rstd = sb("rstd", [P, 2, U])
        dscore = sb("dscore", [P, H, U])
        escore = sb("escore", [P, H, U])
        raw = sb("raw", [P, H, U])
        score = sb("score", [P, H, U + 1])
        cont4 = sb("cont4", [P, H, U + 1])
        peak = sb("peak", [P, H, U + 1])
        args = sb("args", [P, 2, H, U])
        exps = sb("exps", [P, 2, H, U])
        decay4 = sb("decay4", [P, H, U + 1])
        inv = sb("inv", [P, H, U])
        mean = sb("mean", [P, U])
        peak_t = sb("peak_t", [P, H, U])
        head_add = sb("head_add", [P, G + H])
        head_sum = sb("head_sum", [P, G])
        head_peak = sb("head_peak", [P, H])
        R = G * (U + 1)
        decay = nodes[:, 0:R].rearrange("p (g k) -> p g k", g=G)
        terms = nodes[:, R:2 * R].rearrange("p (g k) -> p g k", g=G)
        sums = nodes[:, 2 * R:3 * R].rearrange("p (g k) -> p g k", g=G)

        psT = ctx.enter_context(nc.psum_tensor("psT", [P, 1024], f32))
        psC = ctx.enter_context(nc.psum_tensor("psC", [P, 1024], f32))
        psH = [ctx.enter_context(nc.psum_tensor(f"psH{r}", [P, 1024], f32)) for r in range(2)]

        weights_in = sem("weights_in")
        src_in = sem("src_in")
        dst_in = sem("dst_in")
        attr_in = sem("attr_in")
        nodes_in = [[sem(f"nodes_in{s}{h}") for h in range(2)] for s in range(2)]
        rows_gathered = [sem(f"rows_gathered{s}") for s in range(2)]
        rows_stored = [sem(f"rows_stored{s}") for s in range(2)]
        rows_scattered = [sem(f"rows_scattered{s}") for s in range(2)]
        pads_set = sem("pads_set")
        idx_staged = sem("idx_staged")
        out_idx_staged = sem("out_idx_staged")
        pool_const = sem("pool_const")
        const_ready = sem("const_ready")
        flags_ready = sem("flags_ready")
        turned = sem("turned")
        turned_copied = sem("turned_copied")
        centered = sem("centered")
        relu_ready = sem("relu_ready")
        h_ready = sem("h_ready")
        h_free = sem("h_free")
        h_squared = sem("h_squared")
        var_ready = sem("var_ready")
        std_ready = sem("std_ready")
        rows_done = sem("rows_done")
        args_ready = sem("args_ready")
        exps_ready = sem("exps_ready")
        decay_ready = sem("decay_ready")
        decay_long = sem("decay_long")
        y_centered = sem("y_centered")
        y_squared = sem("y_squared")
        var2_ready = sem("var2_ready")
        std2_ready = sem("std2_ready")
        final_done = sem("final_done")
        dve_steps = sem("dve_steps")
        ends_ready = sem("ends_ready")
        ends_turned = sem("ends_turned")
        fix_args = sem("fix_args")
        fix_exps = sem("fix_exps")
        fix_args2 = sem("fix_args2")
        fix_exps2 = sem("fix_exps2")
        totals_ready = sem("totals_ready")
        totals_turned = sem("totals_turned")
        fix_var = sem("fix_var")
        fix_std = sem("fix_std")
        fix_done = sem("fix_done")
        fix_scattered = sem("fix_scattered")

        block = ctx.enter_context(nc.Block())

        PER_GATHER = 16 * U

        def unit1(s, i):
            if isinstance(s, int) and 6 * s + i >= UNITS:
                return unit2(0, 6 * s + i - UNITS)
            it, k = divmod(i, 3)
            return Unit(s * 6 + i, "node" if k else "src", s * 2 + it, s + it // 2, it % 2, i % 2, max(k - 1, 0))

        def unit2(s, j):
            return Unit(s * 2 + (UNITS + j), "dst", s * 2 + j, s + j // 2, j % 2, j % 2)

        def partition_rows(dram, width):
            return dram[0:(P - 1) * EDGES].rearrange("(p k) -> p k", p=P - 1) if width == 1 else \
                dram[0:(P - 1) * EDGES, :].rearrange("(p k) d -> p k d", p=P - 1)

        x_main = x[0:P * ROWS, :].rearrange("(p j) f -> p (j f)", j=ROWS)
        x_tail = x[P * ROWS:N, :].rearrange("(p j) f -> p (j f)", j=2)
        out_main = out[0:P * ROWS, :].rearrange("(p j) f -> p (j f)", j=ROWS)
        out_tail = out[P * ROWS:N, :].rearrange("(p j) f -> p (j f)", j=2)

        ends = relu[:, :, :].rearrange("p r c -> p (r c)")[:, 0:5 * G].rearrange("p (n g) -> p n g", n=5)
        ends_t = squares[0:G, :, :].rearrange("p r c -> p (r c)")[:, 0:5 * P].rearrange("p (n q) -> p n q", n=5)
        line = xT[0:G, :, :].rearrange("p r c -> p (r c)")[:, 0:12 * (P + 1)].rearrange("p (n q) -> p n q", n=12)
        totals = line[:, 11, 0:P]

        def ends_ps(n):
            return psT[0:G, n * P:(n + 1) * P] if n < 4 else psT[0:G, 512:512 + P]

        @block.sync
        def _(sp):
            def edge_parts(tile, dram, width, done):
                full = partition_rows(dram, width)
                sp.dma_start(tile[0:ROWS_A], full[0:ROWS_A]).then_inc(done, 16)
                sp.dma_start(tile[ROWS_A:P - 1], full[ROWS_A:P - 1]).then_inc(done, 16)
                last = dram[(P - 1) * EDGES:E] if width == 1 else dram[(P - 1) * EDGES:E, :]
                sp.dma_start(tile[P - 1:P, 0:LAST_E], last.unsqueeze(0)).then_inc(done, 16)

            def load_nodes(u):
                to = (2 * u.slot + u.half) * (U * F)
                sp.dma_start(nodes[:, to:to + U * F], x_main[:, bass.ds(u.idx * (DC * F) + u.half * (U * F), U * F)])\
                    .then_inc(nodes_in[u.slot][u.half], 16)

            sp.wait_ge(pads_set, 3)
            edge_parts(src_idx[:, :], src, 1, src_in)
            for i in (1, 2, 4, 5):
                load_nodes(unit1(0, i))
            sp.dma_start(w_two[0:F, :], w_node).then_inc(weights_in, 16)
            sp.dma_start(w_two[F:P, :], w_node).then_inc(weights_in, 16)
            for n, a in enumerate((attn_src, attn_dst)):
                sp.dma_start(attn_b[:, n, :], a.rearrange("h d -> (h d)").partition_broadcast(P)).then_inc(weights_in, 16)
            sp.dma_start(gamma_b[:, :], gamma.partition_broadcast(P)).then_inc(weights_in, 16)
            sp.dma_start(beta_b[:, :], beta.partition_broadcast(P)).then_inc(weights_in, 16)
            sp.dma_start(wedge_b[:, :, :].rearrange("p d h -> p (d h)"),
                         w_edge.rearrange("d h -> (d h)").partition_broadcast(P)).then_inc(weights_in, 16)
            edge_parts(dst_int[:, 1:EDGES + 1], dst, 1, dst_in)
            for to, at in ((dst_int[1:P, 0:1], EDGES - 1), (dst_int[0:P - 1, EDGES + 1:EDGES + 2], EDGES)):
                step = dst[at:at + (P - 2) * EDGES + 1:EDGES]
                sp.dma_start(to, step.unsqueeze(1), allow_slow_non_contiguous=True).then_inc(dst_in, 16)
            edge_parts(attr[:, :, :], edge_attr, ED, attr_in)

            def store(u):
                sp.wait_ge(rows_done, u.idx * 2 + (u.half + 1))
                sp.dma_start(out_main[:, bass.ds(u.idx * (DC * F) + u.half * (U * F), U * F)],
                             done_rows[:, u.half].rearrange("p j f -> p (j f)")).then_inc(rows_stored[u.half], 16)

            with sp.Fori(0, STEPS - 2) as s:
                for i in (1, 2, 4, 5):
                    store(unit1(s, i))
                    load_nodes(unit1(s, i + 6))
            for t in range(CHUNKS - 4, CHUNKS - 1):
                for i in (1, 2):
                    store(unit1(0, 3 * t + i))
                    if t + 2 < CHUNKS - 1:
                        load_nodes(unit1(0, 3 * (t + 2) + i))
                if t + 2 == CHUNKS - 1:
                    base, at = DC * F, (CHUNKS - 1) * DC * F
                    sp.dma_start(nodes[:, base:base + U * F], x_main[:, at:at + U * F]).then_inc(nodes_in[1][0], 16)
                    sp.dma_start(nodes[:, base + U * F:base + REST * F], x_main[:, at + U * F:ROWS * F])\
                        .then_inc(nodes_in[1][1], 16)
                    sp.dma_start(nodes[0:PT, base + REST * F:base + (REST + 2) * F], x_tail).then_inc(nodes_in[1][1], 16)
            at, left = (CHUNKS - 1) * DC * F, REST - U
            store(unit1(0, UNITS - 2))
            sp.wait_ge(rows_done, 2 * CHUNKS)
            sp.dma_start(out_main[:, at + U * F:ROWS * F],
                         done_rows[:, 1, 0:left, :].rearrange("p j f -> p (j f)")).then_inc(rows_stored[1], 16)
            sp.dma_start(out_tail, done_rows[0:PT, 1, left:left + 2, :].rearrange("p j f -> p (j f)"))\
                .then_inc(rows_stored[1], 16)
            for half in range(2):
                sp.wait_ge(rows_stored[half], 16 * (CHUNKS + half))

        @block.gpsimd
        def _(pool):
            def gather(idx, u):
                nc.gpsimd.tensor_copy(idx_now[:, u.slot, :], idx[:, bass.ds(u.idx * U, U)]).then_inc(idx_staged, 1)
                pool.wait_ge(idx_staged, 1)
                pool.sem_clear(idx_staged)
                for k in range(U):
                    nc.gpsimd.indirect_dma_start(
                        out=gathered[:, u.slot, k, :], out_offset=None, in_=x[:, :],
                        in_offset=bass.IndirectOffsetOnAxis(ap=idx_now[:, u.slot, k:k + 1], axis=0),
                        bounds_check=N - 1, oob_is_err=False).then_inc(rows_gathered[u.slot], 16)

            def scatter(u):
                pool.wait_ge(final_done, u.idx + 1)
                nc.gpsimd.tensor_copy(out_idx_now[:, u.slot, :],
                                      scatter_idx[:, bass.ds(u.idx * U, U)]).then_inc(out_idx_staged, 1)
                pool.wait_ge(out_idx_staged, 1)
                pool.sem_clear(out_idx_staged)
                for k in range(U):
                    nc.gpsimd.indirect_dma_start(
                        out=out[:, :],
                        out_offset=bass.IndirectOffsetOnAxis(ap=out_idx_now[:, u.slot, k:k + 1], axis=0),
                        in_=done_rows[:, u.slot, k, :], in_offset=None,
                        bounds_check=N - 1, oob_is_err=False).then_inc(rows_scattered[u.slot], 16)

            pool.wait_ge(src_in, 48)
            gather(src_idx, unit1(0, 0))
            nc.gpsimd.memset(ident[:, :], 0.0).then_inc(pool_const, 1)
            pool.wait_ge(pool_const, 1)
            nc.gpsimd.affine_select(out=ident[:, :], in_=ident[:, :], compare_op=ALU.not_equal, fill=1.0, base=0,
                                    pattern=[[-1, P]], channel_multiplier=1).then_inc(pool_const, 1)
            gather(src_idx, unit1(0, 3))
            with pool.Fori(0, STEPS - 1) as s:
                for i in (6, 9):
                    u = unit1(s, i)
                    pool.wait_ge(turned, u.u - 5)
                    pool.wait_ge(rows_gathered[u.slot], PER_GATHER * u.turn)
                    gather(src_idx, u)
            pool.wait_ge(flags_ready, 1)
            for j in range(2):
                u = unit2(0, j)
                pool.wait_ge(turned, UNITS - 5 + 3 * j)
                pool.wait_ge(rows_gathered[u.slot], PER_GATHER * STEPS)
                gather(gather_idx, u)
            for half in range(2):
                pool.wait_ge(rows_stored[half], 16 * (CHUNKS + half))

            def gather_and_scatter(before, u):
                pool.wait_ge(final_done, before.idx + 1)
                pool.wait_ge(rows_gathered[u.slot], PER_GATHER * (u.turn + STEPS))
                gather(gather_idx, u)
                wait(pool, rows_scattered[u.slot], PER_GATHER * before.turn)
                scatter(before)

            for j in range(2):
                gather_and_scatter(unit2(0, j), unit2(0, j + 2))
            with pool.Fori(1, STEPS - 1) as s:
                for j in range(2):
                    gather_and_scatter(unit2(s, j), unit2(s, j + 2))
            for j in range(CHUNKS - 2, CHUNKS):
                u = unit2(0, j)
                pool.wait_ge(rows_scattered[u.slot], PER_GATHER * u.turn)
                scatter(u)
            pool.wait_ge(fix_done, 1)
            nc.gpsimd.indirect_dma_start(
                out=out[:, :], out_offset=bass.IndirectOffsetOnAxis(ap=fix_idx[:, 0:1], axis=0),
                in_=fix_row[:, :], in_offset=None, bounds_check=N - 1, oob_is_err=False).then_inc(fix_scattered, 16)
            for slot in range(2):
                pool.wait_ge(rows_scattered[slot], PER_GATHER * STEPS)
            pool.wait_ge(fix_scattered, 16)

        @block.tensor
        def _(pe):
            def turn(u):
                if u.kind == "src":
                    pe.wait_ge(rows_gathered[u.slot], PER_GATHER * (u.turn + 1))
                elif u.kind == "dst":
                    pe.wait_ge(rows_gathered[u.slot], PER_GATHER * (u.turn + 1 + STEPS))
                else:
                    last = isinstance(u.idx, int) and u.u == UNITS - 1
                    pe.wait_ge(nodes_in[u.slot][u.half], 16 * (u.turn + 1 + last))
                pe.wait_ge(turned_copied, u.u)
                rows = gathered[:, u.slot] if u.kind != "node" else \
                    nodes_v[:, u.slot, u.half * U:(u.half + 1) * U, :]
                for m in range(U // 2):
                    last = nc.tensor.transpose(psT[:, m * P:(m + 1) * P],
                                               rows[:, 2 * m:2 * m + 2, :].rearrange("p j f -> p (j f)"), ident[:, :])
                last.then_inc(turned, 1)

            def take_mean(u):
                pe.wait_ge(turned_copied, u.u + 1)
                pe.wait_ge(relu_ready, u.u)
                for a in range(0, U * F, 512):
                    b = min(a + 512, U * F)
                    last = nc.tensor.matmul(psC[:, a:b], center[:, :], xT[:, u.ring, a:b], start=True, stop=True)
                last.then_inc(centered, 1)

            def project(u):
                pe.wait_ge(relu_ready, u.u + 1)
                pe.wait_ge(h_free, u.u + 1)
                ps = psH[u.ring]

                def edge_rows(m, first, end):
                    at = 2 * m + first
                    col = at * G if at < UH else BANK + (at - UH) * G
                    w = w_pair_edge[:, int(u.kind == "dst"), first:end].rearrange("p r g -> p (r g)")
                    nc.tensor.matmul(ps[:, col:col + (end - first) * G], relu[:, u.ring, m * P:(m + 1) * P], w,
                                     start=True, stop=True)

                for m in range(U // 2):
                    if u.kind == "node":
                        nc.tensor.matmul(ps[:, m * P:(m + 1) * P], relu[:, u.ring, m * P:(m + 1) * P],
                                         w_pair_centered[:, :], start=True, stop=True)
                    elif 2 * m + 1 == UH:
                        edge_rows(m, 0, 1)
                        edge_rows(m, 1, 2)
                    else:
                        edge_rows(m, 0, 2)
                    last = nc.tensor.matmul(ps[:, SQUARES + 2 * m:SQUARES + 2 * (m + 1)],
                                            squares[:, u.ring, m * P:(m + 1) * P], ones_pair[:, :],
                                            start=True, stop=True)
                last.then_inc(h_ready, 1)

            pe.sem_inc(h_free, 2)
            pe.wait_ge(pool_const, 2)
            turn(unit1(0, 0))
            turn(unit1(0, 1))
            pe.wait_ge(const_ready, 1)
            take_mean(unit1(0, 0))
            with pe.Fori(0, STEPS - 1) as s:
                for i in range(6):
                    turn(unit1(s, i + 2))
                    take_mean(unit1(s, i + 1))
                    project(unit1(s, i))
            for i in range(6):
                if i < 4:
                    turn(unit1(STEPS - 1, i + 2))
                if i < 5:
                    take_mean(unit1(STEPS - 1, i + 1))
                project(unit1(STEPS - 1, i))
            with pe.Fori(0, STEPS) as s:
                for j in range(2):
                    turn(unit2(s, j))
                    take_mean(unit2(s, j))
                    project(unit2(s, j))
            pe.wait_ge(ends_ready, 1)
            for n in range(5):
                last = nc.tensor.transpose(ends_ps(n), ends[:, n, :], ident[:, :])
            last.then_inc(ends_turned, 1)
            pe.wait_ge(totals_ready, 1)
            nc.tensor.transpose(psC[:, 0:G], totals[:, :], ident[0:G, 0:G]).then_inc(totals_turned, 1)

        @block.scalar
        def _(act):
            def copy_turned(u):
                act.wait_ge(turned, u.u + 1)
                nc.scalar.copy(xT[:, u.ring, :], psT[:, 0:U * F]).then_inc(turned_copied, 1)

            def square_and_relu(u):
                act.wait_ge(centered, u.u + 1)
                nc.scalar.square(squares[:, u.ring, :], psC[:, 0:U * F])
                nc.scalar.activation(relu[:, u.ring, :], psC[:, 0:U * F], ACT.Relu).then_inc(relu_ready, 1)

            def square_h(u):
                act.wait_ge(h_ready, u.u + 1)
                if u.kind == "node":
                    nc.scalar.square(work[:, u.ring, :], psH[u.ring][:, 0:U * F]).then_inc(h_squared, 1)

            def root(u):
                act.wait_ge(var_ready, u.u + 1)
                nc.scalar.sqrt(std[:, u.ring, :], var[:, u.ring, :]).then_inc(std_ready, 1)

            def step(s, i):
                root(unit1(s, i - 2))
                copy_turned(unit1(s, i + 1))
                square_and_relu(unit1(s, i))
                square_h(unit1(s, i - 1))

            copy_turned(unit1(0, 0))
            copy_turned(unit1(0, 1))
            square_and_relu(unit1(0, 0))
            copy_turned(unit1(0, 2))
            square_and_relu(unit1(0, 1))
            square_h(unit1(0, 0))
            with act.Fori(0, STEPS - 1) as s:
                for i in range(2, 8):
                    step(s, i)
            for i in range(2, 5):
                step(STEPS - 1, i)
            root(unit1(STEPS - 1, 3))
            square_and_relu(unit1(STEPS - 1, 5))
            square_h(unit1(STEPS - 1, 4))
            root(unit1(STEPS - 1, 4))
            square_h(unit1(STEPS - 1, 5))
            root(unit1(STEPS - 1, 5))

            def chunk(u, ahead):
                root(u)
                act.wait_ge(args_ready, u.idx + 1)
                nc.scalar.activation(exps[:, :, :, :], args[:, :, :, :], ACT.Exp).then_inc(exps_ready, 1)
                act.wait_ge(decay_ready, u.idx + 1)
                for h in range(H):
                    nc.scalar.copy(decay[:, h * HD:(h + 1) * HD, :],
                                   decay4[:, h, :].unsqueeze(1).broadcast_to([P, HD, U + 1]))
                nc.scalar.copy(decay[:, F:G, :], decay4[:, :, :]).then_inc(decay_long, 1)
                if ahead:
                    copy_turned(ahead)
                    square_and_relu(ahead)
                act.wait_ge(y_centered, u.idx + 1)
                nc.scalar.square(work[:, 1, :], done_rows[:, u.slot].rearrange("p j f -> p (j f)")).then_inc(y_squared, 1)
                act.wait_ge(var2_ready, u.idx + 1)
                nc.scalar.sqrt(std[:, 1, :], var[:, 1, :]).then_inc(std2_ready, 1)

            copy_turned(unit2(0, 0))
            square_and_relu(unit2(0, 0))
            with act.Fori(0, STEPS - 1) as s:
                for j in range(2):
                    chunk(unit2(s, j), unit2(s, j + 1))
            chunk(unit2(STEPS - 1, 0), unit2(STEPS - 1, 1))
            chunk(unit2(STEPS - 1, 1), None)
            act.wait_ge(ends_turned, 1)
            nc.scalar.copy(ends_t[:, 0:4, :].rearrange("p n q -> p (n q)"), psT[0:G, 0:512])
            nc.scalar.copy(ends_t[:, 4, :], psT[0:G, 512:512 + P]).then_inc(ends_turned, 1)
            act.wait_ge(fix_args, 1)
            nc.scalar.activation(line[:, 4:6, 0:P], line[:, 2:4, 0:P], ACT.Exp).then_inc(fix_exps, 1)
            act.wait_ge(fix_args2, 1)
            nc.scalar.activation(line[:, 4:6, 0:P], line[:, 2:4, 0:P], ACT.Exp).then_inc(fix_exps2, 1)
            act.wait_ge(fix_var, 1)
            nc.scalar.sqrt(fix_stat[:, 4:5], fix_stat[:, 3:4]).then_inc(fix_std, 1)

        @block.vector
        def _(dve):
            V = nc.vector
            own = Steps(dve, dve_steps)
            link = own.link

            V.memset(src_idx[96:P, :], 0).then_inc(pads_set, 1)
            V.memset(dst_int[:, :], int(NONE)).then_inc(pads_set, 1)
            V.memset(attr[96:P, LAST_E:, :], 0.0).then_inc(pads_set, 1)
            V.memset(center[:, :], 0.0)
            V.memset(w_pair_centered[:, :], 0.0)
            V.memset(w_pair_edge[:, :, :, :], 0.0)
            link(V.memset(ones_pair[:, :], 0.0))
            for r in range(2):
                lo = r * F
                V.memset(center[lo:lo + F, lo:lo + F], -1.0 / F)
                link(V.memset(ones_pair[lo:lo + F, r:r + 1], 1.0))
            dve.wait_ge(pool_const, 2)
            V.tensor_tensor(center[:, :], center[:, :], ident[:, :], ALU.add)
            dve.wait_ge(weights_in, 7 * 16)
            link(V.tensor_reduce(w_row[:, 0:1], w_two[:, :], AX.X, ALU.add))
            V.tensor_scalar(w_row[:, 1:2], w_row[:, 0:1], 1.0 / F, None, ALU.mult)
            for n in range(2):
                V.tensor_tensor(attn_w[:, n, :], w_two[:, :], attn_b[:, n, :], ALU.mult)
            link(V.memset(w_row[:, 2:3], 0.0))
            for r in range(2):
                lo = r * F
                V.tensor_scalar(w_pair_centered[lo:lo + F, lo:lo + F], w_two[lo:lo + F, :],
                                w_row[lo:lo + F, 1:2], None, ALU.subtract)
                for n in range(2):
                    V.tensor_copy(w_pair_edge[lo:lo + F, n, r, 0:F], w_two[lo:lo + F, :])
                    last = V.tensor_reduce(w_pair_edge[lo:lo + F, n, r, F:G],
                                           attn_w[lo:lo + F, n, :].rearrange("p (h d) -> p h d", h=H), AX.X, ALU.add)
            last.then_inc(const_ready, 1)

            dve.wait_ge(dst_in, 5 * 16)
            link(V.tensor_copy(dst_f[:, :], dst_int[:, :]))
            link(V.memset(dst_f[0:1, 0:1], -1.0))
            here, prev, nxt = dst_f[:, 1:EDGES + 1], dst_f[:, 0:EDGES], dst_f[:, 2:EDGES + 2]
            V.tensor_tensor(continues[:, :], here, prev, ALU.is_equal)
            V.tensor_scalar(head[:, 0:EDGES], here, dst_f[:, 0:1], None, ALU.is_equal)
            V.tensor_scalar(gather_idx[:, :], here, float(N - 1), None, ALU.min)
            link(V.tensor_tensor(flag, here, nxt, ALU.not_equal))
            V.memset(continues[:, 0:1], 0.0)
            link(V.memset(head[:, EDGES:EDGES + 1], 0.0))
            V.tensor_tensor(head_end[:, :], head[:, 0:EDGES], head[:, 1:EDGES + 1], ALU.subtract)
            link(V.tensor_tensor(flag, flag, head[:, 0:EDGES], ALU.is_gt))
            link(V.scalar_tensor_tensor(flag, here, NONE, flag, ALU.subtract, ALU.mult))
            V.tensor_scalar(scatter_idx[:, :], flag, NONE, None, ALU.add)
            link(V.tensor_tensor(fix_f[:, 0:1], here[:, EDGES - 1:EDGES], nxt[:, EDGES - 1:EDGES], ALU.is_equal))
            link(V.tensor_tensor(fix_f[:, 1:2], fix_f[:, 0:1], head[:, EDGES - 1:EDGES], ALU.mult))
            link(V.tensor_tensor(fix_f[:, 2:3], head[:, 0:1], fix_f[:, 1:2], ALU.is_gt))
            link(V.scalar_tensor_tensor(fix_f[:, 3:4], here[:, 0:1], NONE, fix_f[:, 2:3], ALU.subtract, ALU.mult))
            V.tensor_scalar(fix_idx[:, :], fix_f[:, 3:4], NONE, None, ALU.add).then_inc(flags_ready, 1)

            def variances(u):
                dve.wait_ge(h_ready, u.u + 1)
                sq = psH[u.ring][:, SQUARES:SQUARES + U]
                if u.kind != "node":
                    V.tensor_scalar(var[:, u.ring, :], sq, 1.0 / F, EPS_LN, ALU.mult, ALU.add).then_inc(var_ready, 1)
                    return
                dve.wait_ge(h_squared, u.idx * 2 + (u.half + 1))
                V.tensor_scalar(part[:, 0, :], sq, EPS_LN / F, EPS_LN * EPS_LN, ALU.mult, ALU.add)
                link(V.tensor_reduce(part[:, 1, :], work[:, u.ring, :].rearrange("p (j f) -> p j f", f=F), AX.X, ALU.add))
                V.scalar_tensor_tensor(var[:, u.ring, :], part[:, 1, :], 1.0 / F, part[:, 0, :],
                                       ALU.mult, ALU.add).then_inc(var_ready, 1)

            def wide(ap, n=F):
                return ap.unsqueeze(2).broadcast_to([P, U, n])

            def every(ap):
                return ap.unsqueeze(1).broadcast_to([P, U, F])

            def edges_of(u):
                return psH[u.ring][:, :].rearrange("p (b c) -> p b c", b=2)[:, :, 0:UH * G]\
                    .rearrange("p b (j g) -> p b j g", g=G)

            def halves(ap):
                return ap.rearrange("p (b j) f -> p b j f", b=2)

            def wide_halves(ap, n):
                return ap.rearrange("p (b j) -> p b j", b=2).unsqueeze(3).broadcast_to([P, 2, UH, n])

            def scale(u):
                dve.wait_ge(std_ready, u.u + 1)
                link(V.reciprocal(rstd[:, u.ring, :], std[:, u.ring, :]))
                if u.kind == "src":
                    at = bass.ds(u.idx * U, U)
                    V.tensor_tensor(halves(src_score[:, at, :]), edges_of(u)[:, :, :, F:G],
                                    wide_halves(rstd[:, u.ring, :], H), ALU.mult)
                    V.tensor_tensor(halves(src_rows[:, at, :]), edges_of(u)[:, :, :, 0:F],
                                    wide_halves(rstd[:, u.ring, :], F), ALU.mult).then_inc(h_free, 1)
                    return
                wait(dve, rows_stored[u.half], 16 * u.idx)
                V.tensor_tensor(done_rows[:, u.half], psH[u.ring][:, 0:U * F].rearrange("p (j f) -> p j f", f=F),
                                wide(rstd[:, u.ring, :]), ALU.mult).then_inc(h_free, 1)

            def add_residual(u):
                if u.kind == "src":
                    return
                y = done_rows[:, u.half]
                x_rows = nodes_v[:, u.slot, u.half * U:(u.half + 1) * U, :]
                dve.wait_ge(h_free, u.u + 3)
                link(V.tensor_tensor(y, y, every(gamma_b[:, :]), ALU.mult))
                link(V.tensor_tensor(y, y, every(beta_b[:, :]), ALU.add))
                V.tensor_tensor(y, y, x_rows, ALU.add).then_inc(rows_done, 1)

            def step(s, i):
                variances(unit1(s, i))
                add_residual(unit1(s, i - 1))
                scale(unit1(s, i))

            variances(unit1(0, 0))
            scale(unit1(0, 0))
            for i in range(1, 7):
                step(0, i)
            with dve.Fori(1, STEPS - 1) as s:
                own.enter(s, 1, 6 + 4 * 3)
                for i in range(1, 7):
                    step(s, i)
                own.leave(STEPS - 2)
            for i in range(1, 6):
                step(STEPS - 1, i)
            add_residual(unit1(STEPS - 1, 5))

            dve.wait_ge(attr_in, 48)
            dve.wait_ge(rows_done, 2 * CHUNKS)
            V.memset(sums, 0.0)
            V.memset(peak[:, :, :], 0.0)
            V.memset(cont4[:, :, :], 0.0)
            V.memset(decay4[:, :, :], 0.0)
            V.memset(head_sum[:, :], 0.0)
            link(V.memset(head_peak[:, :], 0.0))

            def heads(ap):
                return ap.unsqueeze(2).broadcast_to([P, H, HD, U])

            def output(u, n):
                y = done_rows[:, u.slot, :, :]
                agg = work[:, 0, :].rearrange("p (j f) -> p j f", f=F)
                if isinstance(u.idx, int) and u.idx < 2:
                    dve.wait_ge(rows_stored[u.slot], 16 * (CHUNKS + u.slot))
                else:
                    dve.wait_ge(rows_scattered[u.slot], PER_GATHER * u.turn)
                if isinstance(u.idx, int) and u.idx == 0:
                    V.tensor_copy(first_x[:, :], gathered[:, u.slot, 0, :])
                    V.tensor_scalar(first_h[:, :], edges_of(u)[:, 0, 0, 0:F], rstd[:, 0, 0:1], None, ALU.mult)
                V.tensor_tensor(halves(y), edges_of(u)[:, :, :, 0:F], wide_halves(rstd[:, 0, :], F),
                                ALU.mult).then_inc(h_free, 1)
                dve.wait_ge(h_free, u.u + 3)
                link(V.tensor_tensor(y, y, agg, ALU.add))
                link(V.tensor_reduce(mean[:, :], y, AX.X, ALU.add))
                link(V.tensor_scalar(mean[:, :], mean[:, :], 1.0 / F, None, ALU.mult))
                V.tensor_tensor(y, y, wide(mean[:, :]), ALU.subtract).then_inc(y_centered, 1)
                dve.wait_ge(y_squared, n)
                link(V.tensor_reduce(part[:, 1, :], work[:, 1, :].rearrange("p (j f) -> p j f", f=F), AX.X, ALU.add))
                V.tensor_scalar(var[:, 1, :], part[:, 1, :], 1.0 / F, EPS_LN, ALU.mult, ALU.add).then_inc(var2_ready, 1)
                dve.wait_ge(std2_ready, n)
                link(V.reciprocal(rstd[:, 1, :], std[:, 1, :]))
                link(V.tensor_tensor(y, y, wide(rstd[:, 1, :]), ALU.mult))
                link(V.tensor_tensor(y, y, every(gamma_b[:, :]), ALU.mult))
                link(V.tensor_tensor(y, y, every(beta_b[:, :]), ALU.add))
                V.tensor_tensor(y, y, gathered[:, u.slot, :, :], ALU.add).then_inc(final_done, 1)

            def chunk(u):
                at = bass.ds(u.idx * U, U)
                tmp = work[:, 1, :].rearrange("p (k h d) -> p k h d", h=H, d=ED)
                V.tensor_copy(score[:, :, 0:1], peak[:, :, U:U + 1])
                V.tensor_copy(terms[:, :, 0:1], sums[:, :, U:U + 1])
                V.tensor_copy(cont4[:, :, 1:U + 1], continues[:, at].unsqueeze(1).broadcast_to([P, H, U]))
                link(V.tensor_tensor(tmp, attr[:, at, :].unsqueeze(2).broadcast_to([P, U, H, ED]),
                                     wedge_b[:, :, :].rearrange("p d h -> p h d").unsqueeze(1)
                                     .broadcast_to([P, U, H, ED]), ALU.mult))
                link(V.tensor_reduce(escore[:, :, :].rearrange("p h k -> p k h"), tmp, AX.X, ALU.add))
                V.tensor_tensor(raw[:, :, :], src_score[:, at, :].rearrange("p k h -> p h k"), escore[:, :, :], ALU.add)
                variances(u)
                dve.wait_ge(std_ready, u.u + 1)
                link(V.reciprocal(rstd[:, 0, :], std[:, u.ring, :]))
                link(V.tensor_tensor(dscore[:, :, :].rearrange("p h (b j) -> p b j h", b=2),
                                     edges_of(u)[:, :, :, F:G], wide_halves(rstd[:, 0, :], H), ALU.mult))
                link(V.tensor_tensor(raw[:, :, :], raw[:, :, :], dscore[:, :, :], ALU.add))
                link(V.scalar_tensor_tensor(score[:, :, 1:U + 1], raw[:, :, :], NEG_SLOPE, raw[:, :, :],
                                            ALU.mult, ALU.max))
                link(V.tensor_tensor_scan(peak[:, :, :].rearrange("p h k -> p (h k)"),
                                          cont4[:, :, :].rearrange("p h k -> p (h k)"),
                                          score[:, :, :].rearrange("p h k -> p (h k)"), 0.0, ALU.mult, ALU.max))
                V.tensor_tensor(args[:, 0], score[:, :, 1:U + 1], peak[:, :, 1:U + 1], ALU.subtract)
                link(V.tensor_tensor(args[:, 1], peak[:, :, 0:U], peak[:, :, 1:U + 1], ALU.subtract))
                V.tensor_scalar(args[:, 1], args[:, 1], 0.0, None, ALU.min).then_inc(args_ready, 1)
                dve.wait_ge(exps_ready, u.idx + 1)
                V.tensor_tensor(decay4[:, :, 1:U + 1], exps[:, 1], cont4[:, :, 1:U + 1], ALU.mult).then_inc(decay_ready, 1)
                V.tensor_copy(terms[:, F:G, 1:U + 1], exps[:, 0])
                for h in range(H):
                    last = V.tensor_tensor(terms[:, h * HD:(h + 1) * HD, 1:U + 1],
                                           src_rows[:, at, h * HD:(h + 1) * HD].rearrange("p k d -> p d k"),
                                           exps[:, 0, h, :].unsqueeze(1).broadcast_to([P, HD, U]), ALU.mult)
                link(last)
                dve.wait_ge(decay_long, u.idx + 1)
                link(V.tensor_tensor_scan(sums.rearrange("p g k -> p (g k)"), decay.rearrange("p g k -> p (g k)"),
                                          terms.rearrange("p g k -> p (g k)"), 0.0, ALU.mult, ALU.add))
                V.tensor_tensor(decay[:, :, 0:U], sums[:, :, 1:U + 1],
                                head_end[:, at].unsqueeze(1).broadcast_to([P, G, U]), ALU.mult)
                V.tensor_tensor(peak_t[:, :, :], peak[:, :, 1:U + 1],
                                head_end[:, at].unsqueeze(1).broadcast_to([P, H, U]), ALU.mult)
                link(V.tensor_scalar(inv[:, :, :], sums[:, F:G, 1:U + 1], EPS_SOFTMAX, None, ALU.add))
                V.tensor_reduce(head_add[:, 0:G], decay[:, :, 0:U], AX.X, ALU.add)
                V.tensor_reduce(head_add[:, G:G + H], peak_t[:, :, :], AX.X, ALU.add)
                link(V.reciprocal(inv[:, :, :], inv[:, :, :]))
                V.tensor_tensor(head_sum[:, :], head_sum[:, :], head_add[:, 0:G], ALU.add)
                V.tensor_tensor(head_peak[:, :], head_peak[:, :], head_add[:, G:G + H], ALU.add)
                agg = work[:, 0, :].rearrange("p (j f) -> p f j", f=F)
                for h in range(H):
                    last = V.tensor_tensor(agg[:, h * HD:(h + 1) * HD, :], sums[:, h * HD:(h + 1) * HD, 1:U + 1],
                                           inv[:, h, :].unsqueeze(1).broadcast_to([P, HD, U]), ALU.mult)
                link(last)
                output(u, u.idx + 1)

            for j in range(2):
                chunk(unit2(0, j))
            with dve.Fori(1, STEPS) as s:
                own.enter(s, 1, 2 * OWN_CHUNK)
                for j in range(2):
                    chunk(unit2(s, j))
                own.leave(STEPS - 1)

            for h in range(H):
                f0, f1 = h * HD, (h + 1) * HD
                V.tensor_copy(ends[:, 0, f0:f1], peak[:, h, U:U + 1].broadcast_to([P, HD]))
                V.tensor_copy(ends[:, 1, f0:f1], head_peak[:, h:h + 1].broadcast_to([P, HD]))
            V.tensor_copy(ends[:, 0, F:G], peak[:, :, U])
            V.tensor_copy(ends[:, 1, F:G], head_peak[:, :])
            V.tensor_copy(ends[:, 2, :], sums[:, :, U])
            V.tensor_copy(ends[:, 3, :], head_sum[:, :])
            V.tensor_copy(ends[:, 4, :], head[:, EDGES - 1:EDGES].broadcast_to([P, G])).then_inc(ends_ready, 1)
            dve.wait_ge(ends_turned, 2)
            last_peak, head_peak_t, last_sum, head_sum_t, whole = (ends_t[:, n, :] for n in range(5))
            V.memset(line[:, 0:2, 0:1], 0.0)
            link(V.tensor_tensor_scan(line[:, 0, 1:P + 1], whole, last_peak, 0.0, ALU.mult, ALU.max))
            V.tensor_tensor(line[:, 2, 0:P], line[:, 0, 0:P], line[:, 0, 1:P + 1], ALU.subtract)
            link(V.tensor_tensor(line[:, 3, 0:P], last_peak, line[:, 0, 1:P + 1], ALU.subtract))
            V.tensor_scalar(line[:, 2:4, 0:P], line[:, 2:4, 0:P], 0.0, None, ALU.min).then_inc(fix_args, 1)
            dve.wait_ge(fix_exps, 1)
            V.tensor_tensor(line[:, 6, 0:P], line[:, 4, 0:P], whole, ALU.mult)
            link(V.tensor_tensor(line[:, 7, 0:P], line[:, 5, 0:P], last_sum, ALU.mult))
            link(V.tensor_tensor_scan(line[:, 1, 1:P + 1], line[:, 6, 0:P], line[:, 7, 0:P], 0.0, ALU.mult, ALU.add))
            link(V.tensor_tensor(line[:, 8, 0:P], line[:, 0, 0:P], head_peak_t, ALU.max))
            V.tensor_tensor(line[:, 2, 0:P], line[:, 0, 0:P], line[:, 8, 0:P], ALU.subtract)
            V.tensor_tensor(line[:, 3, 0:P], head_peak_t, line[:, 8, 0:P], ALU.subtract).then_inc(fix_args2, 1)
            dve.wait_ge(fix_exps2, 1)
            V.tensor_tensor(line[:, 9, 0:P], line[:, 4, 0:P], line[:, 1, 0:P], ALU.mult)
            link(V.tensor_tensor(line[:, 10, 0:P], line[:, 5, 0:P], head_sum_t, ALU.mult))
            V.tensor_tensor(totals, line[:, 9, 0:P], line[:, 10, 0:P], ALU.add).then_inc(totals_ready, 1)
            dve.wait_ge(totals_turned, 1)
            link(V.tensor_scalar(inv[:, :, 0], psC[:, F:G], EPS_SOFTMAX, None, ALU.add))
            link(V.reciprocal(inv[:, :, 0], inv[:, :, 0]))
            link(V.tensor_tensor(fix_row[:, :].rearrange("p (h d) -> p h d", h=H),
                                 psC[:, 0:F].rearrange("p (h d) -> p h d", h=H),
                                 inv[:, :, 0:1].broadcast_to([P, H, HD]), ALU.mult))
            link(V.tensor_tensor(fix_row[:, :], fix_row[:, :], first_h[:, :], ALU.add))
            link(V.tensor_reduce(fix_stat[:, 0:1], fix_row[:, :], AX.X, ALU.add))
            link(V.tensor_scalar(fix_stat[:, 1:2], fix_stat[:, 0:1], 1.0 / F, None, ALU.mult))
            link(V.tensor_scalar(fix_row[:, :], fix_row[:, :], fix_stat[:, 1:2], None, ALU.subtract))
            link(V.tensor_tensor(fix_tmp[:, :], fix_row[:, :], fix_row[:, :], ALU.mult))
            link(V.tensor_reduce(fix_stat[:, 2:3], fix_tmp[:, :], AX.X, ALU.add))
            V.tensor_scalar(fix_stat[:, 3:4], fix_stat[:, 2:3], 1.0 / F, EPS_LN, ALU.mult, ALU.add).then_inc(fix_var, 1)
            dve.wait_ge(fix_std, 1)
            link(V.reciprocal(fix_stat[:, 5:6], fix_stat[:, 4:5]))
            link(V.scalar_tensor_tensor(fix_row[:, :], fix_row[:, :], fix_stat[:, 5:6], gamma_b[:, :], ALU.mult, ALU.mult))
            link(V.tensor_tensor(fix_row[:, :], fix_row[:, :], beta_b[:, :], ALU.add))
            V.tensor_tensor(fix_row[:, :], fix_row[:, :], first_x[:, :], ALU.add).then_inc(fix_done, 1)


_INS = ['x', 'src', 'dst', 'edge_attr_16', 'L0_gnn_W_node', 'L0_gnn_W_edge', 'L0_gnn_attn_src',
        'L0_gnn_attn_dst', 'L0_gnn_ln_gamma', 'L0_gnn_ln_beta']


def kernel(**inputs):
    import numpy as _np
    import concourse.bacc as _bacc
    from concourse import mybir as _mybir
    from concourse.bass_utils import run_bass_kernel_spmd as _run

    nc = _bacc.Bacc("TRN2", target_bir_lowering=False, num_devices=1)
    arrays, args = {}, []
    for name in _INS:
        a = _np.ascontiguousarray(inputs[name])
        arrays[f"in_{name}_dram"] = a
        args.append(nc.dram_tensor(f"in_{name}_dram", a.shape, _mybir.dt.from_np(a.dtype), kind="ExternalInput").ap())
    out = nc.dram_tensor("out_0_dram", inputs["x"].shape, _mybir.dt.float32, kind="ExternalOutput").ap()
    gnn_layer_kernel(nc, *args, out)
    r = _run(nc, [arrays], core_ids=[0])
    return r.results[0]["out_0_dram"]
```

```python
import concourse.bass as bass
from concourse import mybir
from contextlib import ExitStack


OWN_STEP = 6 + 4 * 3
OWN_CHUNK = 21


class Steps:

    def __init__(self, engine, sem):
        self.engine, self.sem, self.base, self.n = engine, sem, 0, 0

    def enter(self, step, first, per_step):
        self.before, self.per_step = self.base + self.n, per_step
        self.base, self.n = per_step * step + (self.before - per_step * first), 0

    def leave(self, turns):
        assert self.n == self.per_step, (self.n, self.per_step)
        self.base, self.n = self.before + self.per_step * turns, 0

    def link(self, instruction):
        instruction.then_inc(self.sem, 1)
        self.n += 1
        self.engine.wait_ge(self.sem, self.base + self.n)


def wait(engine, sem, value):
    if not (isinstance(value, int) and value <= 0):
        engine.wait_ge(sem, value)


class Unit:

    def __init__(self, u, kind, idx, turn, slot, ring, half=0):
        self.u, self.kind, self.idx, self.turn = u, kind, idx, turn
        self.slot, self.ring, self.half = slot, ring, half


def gnn_layer_kernel(nc, x, src, dst, edge_attr, w_node, w_edge, attn_src, attn_dst, gamma, beta, out):
    f32, i32 = mybir.dt.float32, mybir.dt.int32
    ALU, ACT, AX = mybir.AluOpType, mybir.ActivationFunctionType, mybir.AxisListType

    P = 128
    N, F = x.shape
    E, ED = edge_attr.shape
    H = w_edge.shape[1]
    HD = F // H
    EPS_LN, EPS_SOFTMAX, NEG_SLOPE = 1e-5, 1e-8, 0.2

    U = 14
    EDGES = -(-E // (P * U)) * U
    CHUNKS = EDGES // U
    LAST_E = E - (P - 1) * EDGES
    ROWS = N // P // 2 * 2
    DC = 2 * U
    REST = ROWS - (CHUNKS - 1) * DC
    TAIL = N - P * ROWS
    PT = TAIL // 2
    assert CHUNKS % 2 == 0 and 0 < LAST_E <= EDGES and U < REST and REST + 2 <= DC and TAIL % 2 == 0
    UNITS = 3 * CHUNKS
    SLOTS = 8
    SRC_TURNS, OFF = divmod(CHUNKS, SLOTS)
    FULL_A = LAST_E // U
    assert SLOTS % 2 == 0 and OFF * 2 == SLOTS and FULL_A % 2 == 1 and LAST_E % U
    STEPS = CHUNKS // 2
    ROWS_A = 112
    NONE = float(1 << 20)
    G = F + H
    BANK = 512
    UH = U // 2
    SQUARES = BANK + UH * G
    assert U * F <= SQUARES and SQUARES + U <= 2 * BANK and UH * G <= BANK and UH % 2 == 1

    ctx = ExitStack()
    with ctx:
        def sb(name, shape, dt=f32):
            return ctx.enter_context(nc.sbuf_tensor(name, shape, dt))

        def sem(name):
            return ctx.enter_context(nc.semaphore(name))

        src_rows = sb("src_rows", [P, EDGES, F])
        src_score = sb("src_score", [P, EDGES, H])
        row_idx = sb("row_idx", [P, 2 * EDGES], i32)
        dst_int = sb("dst_int", [P, EDGES + 2], i32)
        dst_f = sb("dst_f", [P, EDGES + 2])
        continues = sb("continues", [P, EDGES])
        head = sb("head", [P, EDGES + 1])
        head_end = sb("head_end", [P, EDGES])
        scatter_idx = sb("scatter_idx", [P, EDGES], i32)
        flag = dst_int[:, 0:EDGES].bitcast(f32)
        fix_idx = sb("fix_idx", [P, 1], i32)
        fix_f = sb("fix_f", [P, 4])
        ident = sb("ident", [P, P])
        center = sb("center", [P, P])
        w_two = sb("w_two", [P, F])
        w_pair_centered = sb("w_pair_centered", [P, P])
        w_row = sb("w_row", [P, 4])
        w_pair_edge = sb("w_pair_edge", [P, 2, 2, G])
        first_h = sb("first_h", [P, F])
        first_x = sb("first_x", [P, F])
        fix_row = sb("fix_row", [P, F])
        fix_tmp = sb("fix_tmp", [P, F])
        fix_stat = sb("fix_stat", [P, 8])
        ones_pair = sb("ones_pair", [P, 2])
        gamma_b = sb("gamma_b", [P, F])
        beta_b = sb("beta_b", [P, F])
        wedge_b = sb("wedge_b", [P, ED, H])
        idx_now = sb("idx_now", [P, SLOTS, U], i32)
        out_idx_now = sb("out_idx_now", [P, SLOTS, U], i32)
        gathered = sb("gathered", [P, SLOTS, U, F])
        attr = sb("attr", [P, 2, U, ED])
        nodes = sb("nodes", [P, 2 * DC * F])
        nodes_v = nodes[:, :].rearrange("p (s j f) -> p s j f", s=2, f=F)
        done_rows = sb("done_rows", [P, 2, U, F])
        xT = sb("xT", [P, 2, U * F])
        squares = sb("squares", [P, 2, U * F])
        relu = sb("relu", [P, 2, U * F])
        attn_b = relu[:, 0, 0:2 * F].rearrange("p (n f) -> p n f", n=2)
        attn_w = relu[:, 1, 0:2 * F].rearrange("p (n f) -> p n f", n=2)
        work = sb("work", [P, 2, U * F])
        var = sb("var", [P, 2, U])
        part = sb("part", [P, 2, U])
        std = sb("std", [P, 2, U])
        rstd = sb("rstd", [P, 2, U])
        dscore = sb("dscore", [P, H, U])
        escore = sb("escore", [P, H, U])
        raw = sb("raw", [P, H, U])
        score = sb("score", [P, H, U + 1])
        cont4 = sb("cont4", [P, H, U + 1])
        peak = sb("peak", [P, H, U + 1])
        args = sb("args", [P, 2, H, U])
        exps = sb("exps", [P, 2, H, U])
        decay4 = sb("decay4", [P, H, U + 1])
        inv = sb("inv", [P, H, U])
        mean = sb("mean", [P, U])
        peak_t = sb("peak_t", [P, H, U])
        head_add = sb("head_add", [P, G + H])
        head_sum = sb("head_sum", [P, G])
        head_peak = sb("head_peak", [P, H])
        R = G * (U + 1)
        decay = nodes[:, 0:R].rearrange("p (g k) -> p g k", g=G)
        terms = nodes[:, R:2 * R].rearrange("p (g k) -> p g k", g=G)
        sums = nodes[:, 2 * R:3 * R].rearrange("p (g k) -> p g k", g=G)

        psT = ctx.enter_context(nc.psum_tensor("psT", [P, 1024], f32))
        psC = ctx.enter_context(nc.psum_tensor("psC", [P, 1024], f32))
        psH = [ctx.enter_context(nc.psum_tensor(f"psH{r}", [P, 1024], f32)) for r in range(2)]

        weights_in = sem("weights_in")
        src_in = sem("src_in")
        dst_in = sem("dst_in")
        attr_in = [sem(f"attr_in{s}") for s in range(2)]
        attr_end_in = sem("attr_end_in")
        nodes_in = [[sem(f"nodes_in{s}{h}") for h in range(2)] for s in range(2)]
        rows_gathered = [sem(f"rows_gathered{s}") for s in range(SLOTS)]
        units_gathered = sem("units_gathered")
        rows_stored = [sem(f"rows_stored{s}") for s in range(2)]
        rows_scattered = [sem(f"rows_scattered{s}") for s in range(SLOTS)]
        pads_set = sem("pads_set")
        idx_staged = sem("idx_staged")
        scatters_begun = sem("scatters_begun")
        pool_const = sem("pool_const")
        const_ready = sem("const_ready")
        flags_ready = sem("flags_ready")
        turned = sem("turned")
        turned_copied = sem("turned_copied")
        centered = sem("centered")
        relu_ready = sem("relu_ready")
        h_ready = sem("h_ready")
        h_free = sem("h_free")
        h_squared = sem("h_squared")
        var_ready = sem("var_ready")
        std_ready = sem("std_ready")
        rows_done = sem("rows_done")
        args_ready = sem("args_ready")
        exps_ready = sem("exps_ready")
        decay_ready = sem("decay_ready")
        decay_long = sem("decay_long")
        y_centered = sem("y_centered")
        y_squared = sem("y_squared")
        var2_ready = sem("var2_ready")
        std2_ready = sem("std2_ready")
        final_done = sem("final_done")
        dve_steps = sem("dve_steps")
        ends_ready = sem("ends_ready")
        ends_turned = sem("ends_turned")
        fix_args = sem("fix_args")
        fix_exps = sem("fix_exps")
        fix_args2 = sem("fix_args2")
        fix_exps2 = sem("fix_exps2")
        totals_ready = sem("totals_ready")
        totals_turned = sem("totals_turned")
        fix_var = sem("fix_var")
        fix_std = sem("fix_std")
        fix_done = sem("fix_done")
        fix_scattered = sem("fix_scattered")

        block = ctx.enter_context(nc.Block())

        PER_GATHER = 16 * U

        def unit1(s, i):
            if isinstance(s, int) and 6 * s + i >= UNITS:
                return unit2(0, 6 * s + i - UNITS)
            it, k = divmod(i, 3)
            return Unit(s * 6 + i, "node" if k else "src", s * 2 + it, s + it // 2, it % 2, i % 2, max(k - 1, 0))

        def unit2(s, j):
            return Unit(s * 2 + (UNITS + j), "dst", s * 2 + j, s + j // 2, j % 2, j % 2)

        attr_main = edge_attr[0:(P - 1) * EDGES, :].rearrange("(p k) d -> p (k d)", p=P - 1)
        attr_last = edge_attr[(P - 1) * EDGES:E, :].rearrange("k d -> (k d)")
        x_main = x[0:P * ROWS, :].rearrange("(p j) f -> p (j f)", j=ROWS)
        x_tail = x[P * ROWS:N, :].rearrange("(p j) f -> p (j f)", j=2)
        out_main = out[0:P * ROWS, :].rearrange("(p j) f -> p (j f)", j=ROWS)
        out_tail = out[P * ROWS:N, :].rearrange("(p j) f -> p (j f)", j=2)

        ends = relu[:, :, :].rearrange("p r c -> p (r c)")[:, 0:5 * G].rearrange("p (n g) -> p n g", n=5)
        ends_t = squares[0:G, :, :].rearrange("p r c -> p (r c)")[:, 0:5 * P].rearrange("p (n q) -> p n q", n=5)
        line = xT[0:G, :, :].rearrange("p r c -> p (r c)")[:, 0:12 * (P + 1)].rearrange("p (n q) -> p n q", n=12)
        totals = line[:, 11, 0:P]

        def gathered_rows(u):
            return gathered[:, bass.ds((u.idx + CHUNKS) % SLOTS, 1)].rearrange("p s k f -> p (s k) f")

        def ends_ps(n):
            return psT[0:G, n * P:(n + 1) * P] if n < 4 else psT[0:G, 512:512 + P]

        @block.sync
        def _(sp):
            def edge_parts(tile, dram, done):
                full = dram[0:(P - 1) * EDGES].rearrange("(p k) -> p k", p=P - 1)
                sp.dma_start(tile[0:ROWS_A], full[0:ROWS_A]).then_inc(done, 16)
                sp.dma_start(tile[ROWS_A:P - 1], full[ROWS_A:P - 1]).then_inc(done, 16)
                sp.dma_start(tile[P - 1:P, 0:LAST_E], dram[(P - 1) * EDGES:E].unsqueeze(0)).then_inc(done, 16)

            def load_attr(u, last_rows):
                to = attr[:, u.slot].rearrange("p k d -> p (k d)")
                cols = bass.ds(u.idx * (U * ED), U * ED)
                sp.dma_start(to[0:ROWS_A], attr_main[0:ROWS_A, cols]).then_inc(attr_in[u.slot], 16)
                sp.dma_start(to[ROWS_A:P - 1], attr_main[ROWS_A:P - 1, cols]).then_inc(attr_in[u.slot], 16)
                if last_rows:
                    sp.dma_start(to[P - 1:P, 0:last_rows * ED],
                                 attr_last[bass.ds(u.idx * (U * ED), last_rows * ED)].unsqueeze(0))\
                        .then_inc(attr_in[u.slot], 16)
                else:
                    sp.sem_inc(attr_in[u.slot], 16)

            def load_nodes(u):
                to = (2 * u.slot + u.half) * (U * F)
                sp.dma_start(nodes[:, to:to + U * F], x_main[:, bass.ds(u.idx * (DC * F) + u.half * (U * F), U * F)])\
                    .then_inc(nodes_in[u.slot][u.half], 16)

            sp.wait_ge(pads_set, 2)
            edge_parts(row_idx[:, 0:EDGES], src, src_in)
            for i in (1, 2, 4, 5):
                load_nodes(unit1(0, i))
            sp.dma_start(w_two[0:F, :], w_node).then_inc(weights_in, 16)
            sp.dma_start(w_two[F:P, :], w_node).then_inc(weights_in, 16)
            for n, a in enumerate((attn_src, attn_dst)):
                sp.dma_start(attn_b[:, n, :], a.rearrange("h d -> (h d)").partition_broadcast(P)).then_inc(weights_in, 16)
            sp.dma_start(gamma_b[:, :], gamma.partition_broadcast(P)).then_inc(weights_in, 16)
            sp.dma_start(beta_b[:, :], beta.partition_broadcast(P)).then_inc(weights_in, 16)
            sp.dma_start(wedge_b[:, :, :].rearrange("p d h -> p (d h)"),
                         w_edge.rearrange("d h -> (d h)").partition_broadcast(P)).then_inc(weights_in, 16)
            for j in range(2):
                load_attr(unit2(0, j), U)
            edge_parts(dst_int[:, 1:EDGES + 1], dst, dst_in)
            for to, at in ((dst_int[1:P, 0:1], EDGES - 1), (dst_int[0:P - 1, EDGES + 1:EDGES + 2], EDGES)):
                step = dst[at:at + (P - 2) * EDGES + 1:EDGES]
                sp.dma_start(to, step.unsqueeze(1), allow_slow_non_contiguous=True).then_inc(dst_in, 16)

            def store(u):
                sp.wait_ge(rows_done, u.idx * 2 + (u.half + 1))
                sp.dma_start(out_main[:, bass.ds(u.idx * (DC * F) + u.half * (U * F), U * F)],
                             done_rows[:, u.half].rearrange("p j f -> p (j f)")).then_inc(rows_stored[u.half], 16)

            with sp.Fori(0, STEPS - 2) as s:
                for i in (1, 2, 4, 5):
                    store(unit1(s, i))
                    load_nodes(unit1(s, i + 6))
            for t in range(CHUNKS - 4, CHUNKS - 1):
                for i in (1, 2):
                    store(unit1(0, 3 * t + i))
                    if t + 2 < CHUNKS - 1:
                        load_nodes(unit1(0, 3 * (t + 2) + i))
                    elif t + 2 == CHUNKS - 1:
                        base, at = DC * F, (CHUNKS - 1) * DC * F
                        if i == 1:
                            sp.dma_start(nodes[:, base:base + U * F], x_main[:, at:at + U * F]).then_inc(nodes_in[1][0], 16)
                            continue
                        sp.dma_start(nodes[:, base + U * F:base + REST * F], x_main[:, at + U * F:ROWS * F])\
                            .then_inc(nodes_in[1][1], 16)
                        sp.dma_start(nodes[0:PT, base + REST * F:base + (REST + 2) * F], x_tail).then_inc(nodes_in[1][1], 16)
            at, left = (CHUNKS - 1) * DC * F, REST - U
            store(unit1(0, UNITS - 2))
            sp.wait_ge(rows_done, 2 * CHUNKS)
            sp.dma_start(out_main[:, at + U * F:ROWS * F],
                         done_rows[:, 1, 0:left, :].rearrange("p j f -> p (j f)")).then_inc(rows_stored[1], 16)
            sp.dma_start(out_tail, done_rows[0:PT, 1, left:left + 2, :].rearrange("p j f -> p (j f)"))\
                .then_inc(rows_stored[1], 16)
            for half in range(2):
                sp.wait_ge(rows_stored[half], 16 * (CHUNKS + half))

            def next_attr(s, last_rows):
                for j in range(2):
                    u = unit2(s, j)
                    sp.wait_ge(args_ready, u.idx - 1)
                    load_attr(u, last_rows[j])

            with sp.Fori(1, FULL_A // 2) as s:
                next_attr(s, (U, U))
            next_attr(FULL_A // 2, (U, LAST_E % U))
            with sp.Fori(FULL_A // 2 + 1, STEPS) as s:
                next_attr(s, (0, 0))

        @block.gpsimd
        def _(pool):
            def group(transfer, meanwhile, at):
                for k in range(U):
                    if k == at:
                        meanwhile()
                    transfer(k)

            def gather(slot, meanwhile, index=None, at=4):
                index = idx_now[:, slot, :] if index is None else index
                group(lambda k: nc.gpsimd.indirect_dma_start(
                    out=gathered[:, slot, k, :], out_offset=None, in_=x[:, :],
                    in_offset=bass.IndirectOffsetOnAxis(ap=index[:, k:k + 1], axis=0),
                    bounds_check=N - 1, oob_is_err=False).then_inc(rows_gathered[slot], 16), meanwhile, at)

            def scatter(slot, index, meanwhile):
                group(lambda k: nc.gpsimd.indirect_dma_start(
                    out=out[:, :],
                    out_offset=bass.IndirectOffsetOnAxis(ap=index[:, k:k + 1], axis=0),
                    in_=gathered[:, slot, k, :], in_offset=None,
                    bounds_check=N - 1, oob_is_err=False).then_inc(rows_scattered[slot], 16), meanwhile, 4)

            def report(turn, slot):
                pool.wait_ge(rows_gathered[slot], (turn + 1) * PER_GATHER)
                pool.sem_inc(units_gathered, 1)

            def stage(now, indices, unit, first, end):
                nc.gpsimd.tensor_copy(now[:, first:end, :].rearrange("p s k -> p (s k)"),
                                      indices[:, bass.ds(unit * U, (end - first) * U)]).then_inc(idx_staged, 1)
                pool.wait_ge(idx_staged, 1)
                pool.sem_clear(idx_staged)

            pool.wait_ge(src_in, 48)
            gather(0, lambda: None, row_idx[:, 0:U])
            nc.gpsimd.memset(ident[:, :], 0.0).then_inc(pool_const, 1)
            pool.wait_ge(pool_const, 1)
            nc.gpsimd.affine_select(out=ident[:, :], in_=ident[:, :], compare_op=ALU.not_equal, fill=1.0, base=0,
                                    pattern=[[-1, P]], channel_multiplier=1).then_inc(pool_const, 1)
            for slot in range(1, SLOTS - 1):
                gather(slot, lambda: report(0, slot - 1), row_idx[:, slot * U:(slot + 1) * U])
            pool.wait_ge(flags_ready, 1)

            def before_turn(turn):
                pool.wait_ge(turned, 3 * SLOTS * (turn - 1) + 1)
                report(turn - 1, SLOTS - 2)
                stage(idx_now, row_idx, turn * SLOTS, 0, SLOTS - 1)

            def within_turn(turn, slot):
                pool.wait_ge(turned, 3 * SLOTS * (turn - 1) + (3 * slot + 4))
                if slot == 0:
                    report(turn - 1, SLOTS - 1)
                    stage(idx_now, row_idx, turn * SLOTS + (SLOTS - 1), SLOTS - 1, SLOTS)
                else:
                    report(turn, slot - 1)

            gather(SLOTS - 1, lambda: before_turn(1), row_idx[:, (SLOTS - 1) * U:SLOTS * U])
            with pool.Fori(1, SRC_TURNS + 1) as turn:
                for slot in range(SLOTS - 1):
                    gather(slot, lambda: within_turn(turn, slot))
                gather(SLOTS - 1, lambda: before_turn(turn + 1))
            for slot in range(OFF - 1):
                gather(slot, lambda: within_turn(SRC_TURNS + 1, slot))
            gather(OFF - 1, lambda: report(SRC_TURNS + 1, OFF - 2))

            stage(out_idx_now, scatter_idx, 1, 0, SLOTS - 1)
            for half in range(2):
                pool.wait_ge(rows_stored[half], 16 * (CHUNKS + half))
            pool.wait_ge(final_done, 1)
            scatter(OFF, scatter_idx[:, 0:U], lambda: None)

            def next_finished(chunk):
                pool.wait_ge(final_done, chunk + 1)
                pool.sem_inc(scatters_begun, 1)

            def while_scattering(turn, place, places):
                pool.wait_ge(rows_scattered[(OFF + place) % SLOTS], (turn + 1) * PER_GATHER)
                before = CHUNKS + SLOTS + place - 1
                report(turn + before // SLOTS, before % SLOTS)
                if place == 0:
                    stage(idx_now, row_idx, turn * SLOTS + (CHUNKS + SLOTS), 0, places)

            def while_gathering(turn, place, places):
                if place == 0 and places == SLOTS:
                    stage(out_idx_now, scatter_idx, turn * SLOTS + SLOTS, SLOTS - 1, SLOTS)
                if place == SLOTS - 1:
                    stage(out_idx_now, scatter_idx, turn * SLOTS + (SLOTS + 1), 0, SLOTS - 1)
                elif place < places - 1:
                    next_finished(turn * SLOTS + (place + 2))

            def scatters_and_gathers(turn, places):
                next_finished(turn * SLOTS + 1)
                for place in range(places):
                    scatter((OFF + place + 1) % SLOTS, out_idx_now[:, place, :],
                            lambda: while_scattering(turn, place, places))
                    gather((OFF + place) % SLOTS, lambda: while_gathering(turn, place, places),
                           idx_now[:, place, :], U - 1)

            turns, left = divmod(CHUNKS - SLOTS, SLOTS)
            with pool.Fori(0, turns) as turn:
                scatters_and_gathers(turn, SLOTS)
            scatters_and_gathers(turns, left)
            for c in range(CHUNKS - SLOTS + 1, CHUNKS):
                def meanwhile():
                    if c == CHUNKS - SLOTS + 1:
                        report(2 * CHUNKS // SLOTS - 1, SLOTS - 1)
                pool.wait_ge(final_done, c + 1)
                scatter((OFF + c) % SLOTS, scatter_idx[:, c * U:(c + 1) * U], meanwhile)
            pool.wait_ge(fix_done, 1)
            nc.gpsimd.indirect_dma_start(
                out=out[:, :], out_offset=bass.IndirectOffsetOnAxis(ap=fix_idx[:, 0:1], axis=0),
                in_=fix_row[:, :], in_offset=None, bounds_check=N - 1, oob_is_err=False).then_inc(fix_scattered, 16)
            for slot in range(SLOTS):
                pool.wait_ge(rows_scattered[slot], (CHUNKS + slot) // SLOTS * PER_GATHER)
            pool.wait_ge(fix_scattered, 16)

        @block.tensor
        def _(pe):
            def turn(u, slot):
                if u.kind != "node":
                    pe.wait_ge(units_gathered, u.idx + (1 if u.kind == "src" else CHUNKS + 1))
                else:
                    last = isinstance(u.idx, int) and u.u == UNITS - 1
                    pe.wait_ge(nodes_in[u.slot][u.half], 16 * (u.turn + 1 + last))
                pe.wait_ge(turned_copied, u.u)
                if u.kind != "node":
                    rows = gathered[:, slot]
                else:
                    rows = nodes_v[:, u.slot, u.half * U:(u.half + 1) * U, :]
                for m in range(U // 2):
                    last = nc.tensor.transpose(psT[:, m * P:(m + 1) * P],
                                               rows[:, 2 * m:2 * m + 2, :].rearrange("p j f -> p (j f)"), ident[:, :])
                last.then_inc(turned, 1)

            def take_mean(u):
                pe.wait_ge(turned_copied, u.u + 1)
                pe.wait_ge(relu_ready, u.u)
                for a in range(0, U * F, 512):
                    b = min(a + 512, U * F)
                    last = nc.tensor.matmul(psC[:, a:b], center[:, :], xT[:, u.ring, a:b], start=True, stop=True)
                last.then_inc(centered, 1)

            def project(u):
                pe.wait_ge(relu_ready, u.u + 1)
                pe.wait_ge(h_free, u.u + 1)
                ps = psH[u.ring]

                def edge_rows(m, first, end):
                    at = 2 * m + first
                    col = at * G if at < UH else BANK + (at - UH) * G
                    w = w_pair_edge[:, int(u.kind == "dst"), first:end].rearrange("p r g -> p (r g)")
                    nc.tensor.matmul(ps[:, col:col + (end - first) * G], relu[:, u.ring, m * P:(m + 1) * P], w,
                                     start=True, stop=True)

                for m in range(U // 2):
                    if u.kind == "node":
                        nc.tensor.matmul(ps[:, m * P:(m + 1) * P], relu[:, u.ring, m * P:(m + 1) * P],
                                         w_pair_centered[:, :], start=True, stop=True)
                    elif 2 * m + 1 == UH:
                        edge_rows(m, 0, 1)
                        edge_rows(m, 1, 2)
                    else:
                        edge_rows(m, 0, 2)
                    last = nc.tensor.matmul(ps[:, SQUARES + 2 * m:SQUARES + 2 * (m + 1)],
                                            squares[:, u.ring, m * P:(m + 1) * P], ones_pair[:, :],
                                            start=True, stop=True)
                last.then_inc(h_ready, 1)

            pe.sem_inc(h_free, 2)
            pe.wait_ge(pool_const, 2)
            turn(unit1(0, 0), 0)
            turn(unit1(0, 1), None)
            pe.wait_ge(const_ready, 1)
            take_mean(unit1(0, 0))
            with pe.Fori(0, SRC_TURNS) as t:
                for i in range(3 * SLOTS):
                    turn(unit1(t * (SLOTS // 2), i + 2), (i + 2) // 3 % SLOTS)
                    take_mean(unit1(t * (SLOTS // 2), i + 1))
                    project(unit1(t * (SLOTS // 2), i))
            for i in range(3 * OFF):
                s = SRC_TURNS * (SLOTS // 2)
                if i + 2 < 3 * OFF:
                    turn(unit1(s, i + 2), (i + 2) // 3)
                if i + 1 < 3 * OFF:
                    take_mean(unit1(s, i + 1))
                project(unit1(s, i))

            def chunk(u, slot):
                turn(u, slot)
                take_mean(u)
                project(u)

            for j in range(OFF):
                chunk(unit2(0, j), OFF + j)
            with pe.Fori(0, SRC_TURNS) as t:
                for j in range(SLOTS):
                    chunk(unit2(t * (SLOTS // 2) + OFF // 2, j), j)
            pe.wait_ge(ends_ready, 1)
            for n in range(5):
                last = nc.tensor.transpose(ends_ps(n), ends[:, n, :], ident[:, :])
            last.then_inc(ends_turned, 1)
            pe.wait_ge(totals_ready, 1)
            nc.tensor.transpose(psC[:, 0:G], totals[:, :], ident[0:G, 0:G]).then_inc(totals_turned, 1)

        @block.scalar
        def _(act):
            def copy_turned(u):
                act.wait_ge(turned, u.u + 1)
                nc.scalar.copy(xT[:, u.ring, :], psT[:, 0:U * F]).then_inc(turned_copied, 1)

            def square_and_relu(u):
                act.wait_ge(centered, u.u + 1)
                nc.scalar.square(squares[:, u.ring, :], psC[:, 0:U * F])
                nc.scalar.activation(relu[:, u.ring, :], psC[:, 0:U * F], ACT.Relu).then_inc(relu_ready, 1)

            def square_h(u):
                act.wait_ge(h_ready, u.u + 1)
                if u.kind == "node":
                    nc.scalar.square(work[:, u.ring, :], psH[u.ring][:, 0:U * F]).then_inc(h_squared, 1)

            def root(u):
                act.wait_ge(var_ready, u.u + 1)
                nc.scalar.sqrt(std[:, u.ring, :], var[:, u.ring, :]).then_inc(std_ready, 1)

            def step(s, i):
                root(unit1(s, i - 2))
                copy_turned(unit1(s, i + 1))
                square_and_relu(unit1(s, i))
                square_h(unit1(s, i - 1))

            copy_turned(unit1(0, 0))
            copy_turned(unit1(0, 1))
            square_and_relu(unit1(0, 0))
            copy_turned(unit1(0, 2))
            square_and_relu(unit1(0, 1))
            square_h(unit1(0, 0))
            with act.Fori(0, STEPS - 1) as s:
                for i in range(2, 8):
                    step(s, i)
            for i in range(2, 5):
                step(STEPS - 1, i)
            root(unit1(STEPS - 1, 3))
            square_and_relu(unit1(STEPS - 1, 5))
            square_h(unit1(STEPS - 1, 4))
            root(unit1(STEPS - 1, 4))
            square_h(unit1(STEPS - 1, 5))
            root(unit1(STEPS - 1, 5))

            def chunk(u, ahead):
                root(u)
                act.wait_ge(args_ready, u.idx + 1)
                nc.scalar.activation(exps[:, :, :, :], args[:, :, :, :], ACT.Exp).then_inc(exps_ready, 1)
                act.wait_ge(decay_ready, u.idx + 1)
                for h in range(H):
                    nc.scalar.copy(decay[:, h * HD:(h + 1) * HD, :],
                                   decay4[:, h, :].unsqueeze(1).broadcast_to([P, HD, U + 1]))
                nc.scalar.copy(decay[:, F:G, :], decay4[:, :, :]).then_inc(decay_long, 1)
                if ahead:
                    copy_turned(ahead)
                    square_and_relu(ahead)
                act.wait_ge(y_centered, u.idx + 1)
                nc.scalar.square(work[:, 1, :], done_rows[:, u.slot].rearrange("p j f -> p (j f)")).then_inc(y_squared, 1)
                act.wait_ge(var2_ready, u.idx + 1)
                nc.scalar.sqrt(std[:, 1, :], var[:, 1, :]).then_inc(std2_ready, 1)

            copy_turned(unit2(0, 0))
            square_and_relu(unit2(0, 0))
            with act.Fori(0, STEPS - 1) as s:
                for j in range(2):
                    chunk(unit2(s, j), unit2(s, j + 1))
            chunk(unit2(STEPS - 1, 0), unit2(STEPS - 1, 1))
            chunk(unit2(STEPS - 1, 1), None)
            act.wait_ge(ends_turned, 1)
            nc.scalar.copy(ends_t[:, 0:4, :].rearrange("p n q -> p (n q)"), psT[0:G, 0:512])
            nc.scalar.copy(ends_t[:, 4, :], psT[0:G, 512:512 + P]).then_inc(ends_turned, 1)
            act.wait_ge(fix_args, 1)
            nc.scalar.activation(line[:, 4:6, 0:P], line[:, 2:4, 0:P], ACT.Exp).then_inc(fix_exps, 1)
            act.wait_ge(fix_args2, 1)
            nc.scalar.activation(line[:, 4:6, 0:P], line[:, 2:4, 0:P], ACT.Exp).then_inc(fix_exps2, 1)
            act.wait_ge(fix_var, 1)
            nc.scalar.sqrt(fix_stat[:, 4:5], fix_stat[:, 3:4]).then_inc(fix_std, 1)

        @block.vector
        def _(dve):
            V = nc.vector
            own = Steps(dve, dve_steps)
            link = own.link

            V.memset(row_idx[96:P, 0:EDGES], 0).then_inc(pads_set, 1)
            V.memset(dst_int[:, :], int(NONE)).then_inc(pads_set, 1)
            V.memset(center[:, :], 0.0)
            V.memset(w_pair_centered[:, :], 0.0)
            V.memset(w_pair_edge[:, :, :, :], 0.0)
            link(V.memset(ones_pair[:, :], 0.0))
            for r in range(2):
                lo = r * F
                V.memset(center[lo:lo + F, lo:lo + F], -1.0 / F)
                link(V.memset(ones_pair[lo:lo + F, r:r + 1], 1.0))
            dve.wait_ge(pool_const, 2)
            V.tensor_tensor(center[:, :], center[:, :], ident[:, :], ALU.add)
            dve.wait_ge(weights_in, 7 * 16)
            link(V.tensor_reduce(w_row[:, 0:1], w_two[:, :], AX.X, ALU.add))
            V.tensor_scalar(w_row[:, 1:2], w_row[:, 0:1], 1.0 / F, None, ALU.mult)
            for n in range(2):
                V.tensor_tensor(attn_w[:, n, :], w_two[:, :], attn_b[:, n, :], ALU.mult)
            link(V.memset(w_row[:, 2:3], 0.0))
            for r in range(2):
                lo = r * F
                V.tensor_scalar(w_pair_centered[lo:lo + F, lo:lo + F], w_two[lo:lo + F, :],
                                w_row[lo:lo + F, 1:2], None, ALU.subtract)
                for n in range(2):
                    V.tensor_copy(w_pair_edge[lo:lo + F, n, r, 0:F], w_two[lo:lo + F, :])
                    last = V.tensor_reduce(w_pair_edge[lo:lo + F, n, r, F:G],
                                           attn_w[lo:lo + F, n, :].rearrange("p (h d) -> p h d", h=H), AX.X, ALU.add)
            last.then_inc(const_ready, 1)

            V.memset(peak[:, :, :], 0.0)
            V.memset(cont4[:, :, :], 0.0)
            V.memset(decay4[:, :, :], 0.0)
            V.memset(head_sum[:, :], 0.0)
            V.memset(head_peak[:, :], 0.0)

            dve.wait_ge(dst_in, 5 * 16)
            link(V.tensor_copy(dst_f[:, :], dst_int[:, :]))
            link(V.memset(dst_f[0:1, 0:1], -1.0))
            here, prev, nxt = dst_f[:, 1:EDGES + 1], dst_f[:, 0:EDGES], dst_f[:, 2:EDGES + 2]
            V.tensor_tensor(continues[:, :], here, prev, ALU.is_equal)
            V.tensor_scalar(head[:, 0:EDGES], here, dst_f[:, 0:1], None, ALU.is_equal)
            V.tensor_scalar(row_idx[:, EDGES:2 * EDGES], here, float(N - 1), None, ALU.min)
            link(V.tensor_tensor(flag, here, nxt, ALU.not_equal))
            V.memset(continues[:, 0:1], 0.0)
            link(V.memset(head[:, EDGES:EDGES + 1], 0.0))
            V.tensor_tensor(head_end[:, :], head[:, 0:EDGES], head[:, 1:EDGES + 1], ALU.subtract)
            link(V.tensor_tensor(flag, flag, head[:, 0:EDGES], ALU.is_gt))
            link(V.scalar_tensor_tensor(flag, here, NONE, flag, ALU.subtract, ALU.mult))
            V.tensor_scalar(scatter_idx[:, :], flag, NONE, None, ALU.add)
            link(V.tensor_tensor(fix_f[:, 0:1], here[:, EDGES - 1:EDGES], nxt[:, EDGES - 1:EDGES], ALU.is_equal))
            link(V.tensor_tensor(fix_f[:, 1:2], fix_f[:, 0:1], head[:, EDGES - 1:EDGES], ALU.mult))
            link(V.tensor_tensor(fix_f[:, 2:3], head[:, 0:1], fix_f[:, 1:2], ALU.is_gt))
            link(V.scalar_tensor_tensor(fix_f[:, 3:4], here[:, 0:1], NONE, fix_f[:, 2:3], ALU.subtract, ALU.mult))
            V.tensor_scalar(fix_idx[:, :], fix_f[:, 3:4], NONE, None, ALU.add).then_inc(flags_ready, 1)

            def variances(u):
                dve.wait_ge(h_ready, u.u + 1)
                sq = psH[u.ring][:, SQUARES:SQUARES + U]
                if u.kind != "node":
                    V.tensor_scalar(var[:, u.ring, :], sq, 1.0 / F, EPS_LN, ALU.mult, ALU.add).then_inc(var_ready, 1)
                    return
                dve.wait_ge(h_squared, u.idx * 2 + (u.half + 1))
                V.tensor_scalar(part[:, 0, :], sq, EPS_LN / F, EPS_LN * EPS_LN, ALU.mult, ALU.add)
                link(V.tensor_reduce(part[:, 1, :], work[:, u.ring, :].rearrange("p (j f) -> p j f", f=F), AX.X, ALU.add))
                V.scalar_tensor_tensor(var[:, u.ring, :], part[:, 1, :], 1.0 / F, part[:, 0, :],
                                       ALU.mult, ALU.add).then_inc(var_ready, 1)

            def wide(ap, n=F):
                return ap.unsqueeze(2).broadcast_to([P, U, n])

            def every(ap):
                return ap.unsqueeze(1).broadcast_to([P, U, F])

            def edges_of(u):
                return psH[u.ring][:, :].rearrange("p (b c) -> p b c", b=2)[:, :, 0:UH * G]\
                    .rearrange("p b (j g) -> p b j g", g=G)

            def halves(ap):
                return ap.rearrange("p (b j) f -> p b j f", b=2)

            def wide_halves(ap, n):
                return ap.rearrange("p (b j) -> p b j", b=2).unsqueeze(3).broadcast_to([P, 2, UH, n])

            def scale(u):
                dve.wait_ge(std_ready, u.u + 1)
                link(V.reciprocal(rstd[:, u.ring, :], std[:, u.ring, :]))
                if u.kind == "src":
                    at = bass.ds(u.idx * U, U)
                    V.tensor_tensor(halves(src_score[:, at, :]), edges_of(u)[:, :, :, F:G],
                                    wide_halves(rstd[:, u.ring, :], H), ALU.mult)
                    V.tensor_tensor(halves(src_rows[:, at, :]), edges_of(u)[:, :, :, 0:F],
                                    wide_halves(rstd[:, u.ring, :], F), ALU.mult).then_inc(h_free, 1)
                    return
                wait(dve, rows_stored[u.half], 16 * u.idx)
                V.tensor_tensor(done_rows[:, u.half], psH[u.ring][:, 0:U * F].rearrange("p (j f) -> p j f", f=F),
                                wide(rstd[:, u.ring, :]), ALU.mult).then_inc(h_free, 1)

            def add_residual(u):
                if u.kind == "src":
                    return
                y = done_rows[:, u.half]
                x_rows = nodes_v[:, u.slot, u.half * U:(u.half + 1) * U, :]
                dve.wait_ge(h_free, u.u + 3)
                link(V.tensor_tensor(y, y, every(gamma_b[:, :]), ALU.mult))
                link(V.tensor_tensor(y, y, every(beta_b[:, :]), ALU.add))
                V.tensor_tensor(y, y, x_rows, ALU.add).then_inc(rows_done, 1)

            def step(s, i):
                variances(unit1(s, i))
                add_residual(unit1(s, i - 1))
                scale(unit1(s, i))

            variances(unit1(0, 0))
            scale(unit1(0, 0))
            for i in range(1, 7):
                step(0, i)
            with dve.Fori(1, STEPS - 1) as s:
                own.enter(s, 1, OWN_STEP)
                for i in range(1, 7):
                    step(s, i)
                own.leave(STEPS - 2)
            for i in range(1, 6):
                step(STEPS - 1, i)
            add_residual(unit1(STEPS - 1, 5))

            dve.wait_ge(rows_done, 2 * CHUNKS)
            link(V.memset(sums[:, :, U:U + 1], 0.0))

            def heads(ap):
                return ap.unsqueeze(2).broadcast_to([P, H, HD, U])

            def output(u, n):
                y = done_rows[:, u.slot, :, :]
                agg = work[:, 0, :].rearrange("p (j f) -> p j f", f=F)
                if isinstance(u.idx, int) and u.idx < 2:
                    dve.wait_ge(rows_stored[u.slot], 16 * (CHUNKS + u.slot))
                if isinstance(u.idx, int) and u.idx == 0:
                    V.tensor_copy(first_x[:, :], gathered[:, OFF, 0, :])
                    V.tensor_scalar(first_h[:, :], edges_of(u)[:, 0, 0, 0:F], rstd[:, 0, 0:1], None, ALU.mult)
                V.tensor_tensor(halves(y), edges_of(u)[:, :, :, 0:F], wide_halves(rstd[:, 0, :], F),
                                ALU.mult).then_inc(h_free, 1)
                dve.wait_ge(h_free, u.u + 3)
                link(V.tensor_tensor(y, y, agg, ALU.add))
                link(V.tensor_reduce(mean[:, :], y, AX.X, ALU.add))
                link(V.tensor_scalar(mean[:, :], mean[:, :], 1.0 / F, None, ALU.mult))
                V.tensor_tensor(y, y, wide(mean[:, :]), ALU.subtract).then_inc(y_centered, 1)
                dve.wait_ge(y_squared, n)
                link(V.tensor_reduce(part[:, 1, :], work[:, 1, :].rearrange("p (j f) -> p j f", f=F), AX.X, ALU.add))
                V.tensor_scalar(var[:, 1, :], part[:, 1, :], 1.0 / F, EPS_LN, ALU.mult, ALU.add).then_inc(var2_ready, 1)
                dve.wait_ge(std2_ready, n)
                link(V.reciprocal(rstd[:, 1, :], std[:, 1, :]))
                link(V.tensor_tensor(y, y, wide(rstd[:, 1, :]), ALU.mult))
                link(V.tensor_tensor(y, y, every(gamma_b[:, :]), ALU.mult))
                link(V.tensor_tensor(y, y, every(beta_b[:, :]), ALU.add))
                V.tensor_tensor(gathered_rows(u), y, gathered_rows(u), ALU.add).then_inc(final_done, 1)

            def chunk(u):
                at = bass.ds(u.idx * U, U)
                V.tensor_copy(score[:, :, 0:1], peak[:, :, U:U + 1])
                V.tensor_copy(terms[:, :, 0:1], sums[:, :, U:U + 1])
                V.tensor_copy(cont4[:, :, 1:U + 1], continues[:, at].unsqueeze(1).broadcast_to([P, H, U]))
                tmp = work[:, 1, :].rearrange("p (k h d) -> p k h d", h=H, d=ED)
                dve.wait_ge(attr_in[u.slot], 48 * (u.turn + 1))
                link(V.tensor_tensor(tmp, attr[:, u.slot].unsqueeze(2).broadcast_to([P, U, H, ED]),
                                     wedge_b[:, :, :].rearrange("p d h -> p h d").unsqueeze(1)
                                     .broadcast_to([P, U, H, ED]), ALU.mult))
                link(V.tensor_reduce(escore[:, :, :].rearrange("p h k -> p k h"), tmp, AX.X, ALU.add))
                V.tensor_tensor(raw[:, :, :], src_score[:, at, :].rearrange("p k h -> p h k"), escore[:, :, :], ALU.add)
                variances(u)
                dve.wait_ge(std_ready, u.u + 1)
                link(V.reciprocal(rstd[:, 0, :], std[:, u.ring, :]))
                link(V.tensor_tensor(dscore[:, :, :].rearrange("p h (b j) -> p b j h", b=2),
                                     edges_of(u)[:, :, :, F:G], wide_halves(rstd[:, 0, :], H), ALU.mult))
                link(V.tensor_tensor(raw[:, :, :], raw[:, :, :], dscore[:, :, :], ALU.add))
                link(V.scalar_tensor_tensor(score[:, :, 1:U + 1], raw[:, :, :], NEG_SLOPE, raw[:, :, :],
                                            ALU.mult, ALU.max))
                link(V.tensor_tensor_scan(peak[:, :, :].rearrange("p h k -> p (h k)"),
                                          cont4[:, :, :].rearrange("p h k -> p (h k)"),
                                          score[:, :, :].rearrange("p h k -> p (h k)"), 0.0, ALU.mult, ALU.max))
                V.tensor_tensor(args[:, 0], score[:, :, 1:U + 1], peak[:, :, 1:U + 1], ALU.subtract)
                link(V.tensor_tensor(args[:, 1], peak[:, :, 0:U], peak[:, :, 1:U + 1], ALU.subtract))
                V.tensor_scalar(args[:, 1], args[:, 1], 0.0, None, ALU.min).then_inc(args_ready, 1)
                dve.wait_ge(exps_ready, u.idx + 1)
                V.tensor_tensor(decay4[:, :, 1:U + 1], exps[:, 1], cont4[:, :, 1:U + 1], ALU.mult).then_inc(decay_ready, 1)
                V.tensor_copy(terms[:, F:G, 1:U + 1], exps[:, 0])
                for h in range(H):
                    last = V.tensor_tensor(terms[:, h * HD:(h + 1) * HD, 1:U + 1],
                                           src_rows[:, at, h * HD:(h + 1) * HD].rearrange("p k d -> p d k"),
                                           exps[:, 0, h, :].unsqueeze(1).broadcast_to([P, HD, U]), ALU.mult)
                link(last)
                dve.wait_ge(decay_long, u.idx + 1)
                link(V.tensor_tensor_scan(sums.rearrange("p g k -> p (g k)"), decay.rearrange("p g k -> p (g k)"),
                                          terms.rearrange("p g k -> p (g k)"), 0.0, ALU.mult, ALU.add))
                V.tensor_tensor(decay[:, :, 0:U], sums[:, :, 1:U + 1],
                                head_end[:, at].unsqueeze(1).broadcast_to([P, G, U]), ALU.mult)
                V.tensor_tensor(peak_t[:, :, :], peak[:, :, 1:U + 1],
                                head_end[:, at].unsqueeze(1).broadcast_to([P, H, U]), ALU.mult)
                link(V.tensor_scalar(inv[:, :, :], sums[:, F:G, 1:U + 1], EPS_SOFTMAX, None, ALU.add))
                V.tensor_reduce(head_add[:, 0:G], decay[:, :, 0:U], AX.X, ALU.add)
                V.tensor_reduce(head_add[:, G:G + H], peak_t[:, :, :], AX.X, ALU.add)
                link(V.reciprocal(inv[:, :, :], inv[:, :, :]))
                V.tensor_tensor(head_sum[:, :], head_sum[:, :], head_add[:, 0:G], ALU.add)
                V.tensor_tensor(head_peak[:, :], head_peak[:, :], head_add[:, G:G + H], ALU.add)
                agg = work[:, 0, :].rearrange("p (j f) -> p f j", f=F)
                for h in range(H):
                    last = V.tensor_tensor(agg[:, h * HD:(h + 1) * HD, :], sums[:, h * HD:(h + 1) * HD, 1:U + 1],
                                           inv[:, h, :].unsqueeze(1).broadcast_to([P, HD, U]), ALU.mult)
                link(last)
                output(u, u.idx + 1)

            for j in range(2):
                chunk(unit2(0, j))
            with dve.Fori(1, STEPS) as s:
                own.enter(s, 1, 2 * OWN_CHUNK)
                for j in range(2):
                    chunk(unit2(s, j))
                own.leave(STEPS - 1)

            for h in range(H):
                f0, f1 = h * HD, (h + 1) * HD
                V.tensor_copy(ends[:, 0, f0:f1], peak[:, h, U:U + 1].broadcast_to([P, HD]))
                V.tensor_copy(ends[:, 1, f0:f1], head_peak[:, h:h + 1].broadcast_to([P, HD]))
            V.tensor_copy(ends[:, 0, F:G], peak[:, :, U])
            V.tensor_copy(ends[:, 1, F:G], head_peak[:, :])
            V.tensor_copy(ends[:, 2, :], sums[:, :, U])
            V.tensor_copy(ends[:, 3, :], head_sum[:, :])
            V.tensor_copy(ends[:, 4, :], head[:, EDGES - 1:EDGES].broadcast_to([P, G])).then_inc(ends_ready, 1)
            dve.wait_ge(ends_turned, 2)
            last_peak, head_peak_t, last_sum, head_sum_t, whole = (ends_t[:, n, :] for n in range(5))
            V.memset(line[:, 0:2, 0:1], 0.0)
            link(V.tensor_tensor_scan(line[:, 0, 1:P + 1], whole, last_peak, 0.0, ALU.mult, ALU.max))
            V.tensor_tensor(line[:, 2, 0:P], line[:, 0, 0:P], line[:, 0, 1:P + 1], ALU.subtract)
            link(V.tensor_tensor(line[:, 3, 0:P], last_peak, line[:, 0, 1:P + 1], ALU.subtract))
            V.tensor_scalar(line[:, 2:4, 0:P], line[:, 2:4, 0:P], 0.0, None, ALU.min).then_inc(fix_args, 1)
            dve.wait_ge(fix_exps, 1)
            V.tensor_tensor(line[:, 6, 0:P], line[:, 4, 0:P], whole, ALU.mult)
            link(V.tensor_tensor(line[:, 7, 0:P], line[:, 5, 0:P], last_sum, ALU.mult))
            link(V.tensor_tensor_scan(line[:, 1, 1:P + 1], line[:, 6, 0:P], line[:, 7, 0:P], 0.0, ALU.mult, ALU.add))
            link(V.tensor_tensor(line[:, 8, 0:P], line[:, 0, 0:P], head_peak_t, ALU.max))
            V.tensor_tensor(line[:, 2, 0:P], line[:, 0, 0:P], line[:, 8, 0:P], ALU.subtract)
            V.tensor_tensor(line[:, 3, 0:P], head_peak_t, line[:, 8, 0:P], ALU.subtract).then_inc(fix_args2, 1)
            dve.wait_ge(fix_exps2, 1)
            V.tensor_tensor(line[:, 9, 0:P], line[:, 4, 0:P], line[:, 1, 0:P], ALU.mult)
            link(V.tensor_tensor(line[:, 10, 0:P], line[:, 5, 0:P], head_sum_t, ALU.mult))
            V.tensor_tensor(totals, line[:, 9, 0:P], line[:, 10, 0:P], ALU.add).then_inc(totals_ready, 1)
            dve.wait_ge(totals_turned, 1)
            link(V.tensor_scalar(inv[:, :, 0], psC[:, F:G], EPS_SOFTMAX, None, ALU.add))
            link(V.reciprocal(inv[:, :, 0], inv[:, :, 0]))
            link(V.tensor_tensor(fix_row[:, :].rearrange("p (h d) -> p h d", h=H),
                                 psC[:, 0:F].rearrange("p (h d) -> p h d", h=H),
                                 inv[:, :, 0:1].broadcast_to([P, H, HD]), ALU.mult))
            link(V.tensor_tensor(fix_row[:, :], fix_row[:, :], first_h[:, :], ALU.add))
            link(V.tensor_reduce(fix_stat[:, 0:1], fix_row[:, :], AX.X, ALU.add))
            link(V.tensor_scalar(fix_stat[:, 1:2], fix_stat[:, 0:1], 1.0 / F, None, ALU.mult))
            link(V.tensor_scalar(fix_row[:, :], fix_row[:, :], fix_stat[:, 1:2], None, ALU.subtract))
            link(V.tensor_tensor(fix_tmp[:, :], fix_row[:, :], fix_row[:, :], ALU.mult))
            link(V.tensor_reduce(fix_stat[:, 2:3], fix_tmp[:, :], AX.X, ALU.add))
            V.tensor_scalar(fix_stat[:, 3:4], fix_stat[:, 2:3], 1.0 / F, EPS_LN, ALU.mult, ALU.add).then_inc(fix_var, 1)
            dve.wait_ge(fix_std, 1)
            link(V.reciprocal(fix_stat[:, 5:6], fix_stat[:, 4:5]))
            link(V.scalar_tensor_tensor(fix_row[:, :], fix_row[:, :], fix_stat[:, 5:6], gamma_b[:, :], ALU.mult, ALU.mult))
            link(V.tensor_tensor(fix_row[:, :], fix_row[:, :], beta_b[:, :], ALU.add))
            V.tensor_tensor(fix_row[:, :], fix_row[:, :], first_x[:, :], ALU.add).then_inc(fix_done, 1)


_INS = ['x', 'src', 'dst', 'edge_attr_16', 'L0_gnn_W_node', 'L0_gnn_W_edge', 'L0_gnn_attn_src',
        'L0_gnn_attn_dst', 'L0_gnn_ln_gamma', 'L0_gnn_ln_beta']


def kernel(**inputs):
    import numpy as _np
    import concourse.bacc as _bacc
    from concourse import mybir as _mybir
    from concourse.bass_utils import run_bass_kernel_spmd as _run

    nc = _bacc.Bacc("TRN2", target_bir_lowering=False, num_devices=1)
    arrays, args = {}, []
    for name in _INS:
        a = _np.ascontiguousarray(inputs[name])
        arrays[f"in_{name}_dram"] = a
        args.append(nc.dram_tensor(f"in_{name}_dram", a.shape, _mybir.dt.from_np(a.dtype), kind="ExternalInput").ap())
    out = nc.dram_tensor("out_0_dram", inputs["x"].shape, _mybir.dt.float32, kind="ExternalOutput").ap()
    gnn_layer_kernel(nc, *args, out)
    r = _run(nc, [arrays], core_ids=[0])
    return r.results[0]["out_0_dram"]
```
